# Optimizing a Trainium2 kernel written in Bass

```python
import numpy as np
import jax
import jax.numpy as jnp

def _softmax(x, axis=-1):
    return jax.nn.softmax(x, axis=axis)

def _gelu(x):
    return jax.nn.gelu(x, approximate=True)

def _silu(x):
    return jax.nn.silu(x)

def _sigmoid(x):
    return jax.nn.sigmoid(x)

def _layernorm(x, axis=-1, eps=1e-05):
    m = jnp.mean(x, axis=axis, keepdims=True)
    v = jnp.var(x, axis=axis, keepdims=True)
    return (x - m) / jnp.sqrt(v + eps)

def _scatter_add(tgt, idx, src, axis=0):
    return tgt.at[idx].add(src)

def _segment_sum(src, seg, n):
    return jax.ops.segment_sum(src, seg, n)
kernel_name = 'mk_adj_resnorm_d2_adj_r2_471c99'

def setup_inputs(seed: int=0):
    np.random.seed(seed)
    _w = jnp.asarray

    def _rec_inputs():
        import jax
        import jax.numpy as jnp
        _gk = jax.random.key(seed)
        x = -0.001003 + 1 * jax.random.normal(jax.random.fold_in(_gk, 1), (4096, 256), jnp.float32)
        _a = jax.random.bernoulli(jax.random.fold_in(_gk, 2), 0.000488281, (4096, 4096))
        _a = jnp.logical_or(_a, jnp.swapaxes(_a, -1, -2))
        _a = jnp.logical_or(_a, jnp.eye(4096, dtype=bool))
        _af = _a.astype(jnp.float32)
        adj = _af
        return (x, adj)
    x, adj = _rec_inputs()

    def _L0_gnn_setup():
        import jax, jax.numpy as jnp
        import numpy as np
        N, F, H = (1536, 256, 4)
        D = F // H
        ALPHA = 0.5
        EPS = 1e-06

        def _batchnorm(x, gamma, beta):
            m = jnp.mean(x, axis=0)
            v = jnp.var(x, axis=0)
            return (x - m) * jax.lax.rsqrt(v + EPS) * gamma + beta

        def _masked_softmax(scores, mask):
            s = jnp.where(mask, scores, -jnp.inf)
            att = jax.nn.softmax(s, axis=-1)
            return jnp.where(mask, att, 0.0)

        def _mlp_block(x, Wm, bm, g, b):
            h = jax.nn.elu(x @ Wm.T + bm) + x
            return _batchnorm(h, g, b)
        key = jax.random.key(seed)
        ks = jax.random.split(key, 12)
        X = jax.random.normal(ks[0], (N, F), dtype=jnp.float32)
        eye = jnp.eye(N, dtype=jnp.float32)
        local = (jax.random.uniform(ks[1], (N, N)) < 32.0 / N).astype(jnp.float32)
        local = jnp.clip(local + eye, 0.0, 1.0)
        longr = (jax.random.uniform(ks[2], (N, N)) < 16.0 / N).astype(jnp.float32)
        longr = jnp.clip(longr + eye, 0.0, 1.0)
        W = jax.random.normal(ks[3], (H, D, D), dtype=jnp.float32) * 0.1
        V = jax.random.normal(ks[4], (H, 2, D, 1), dtype=jnp.float32) * 0.1
        return {'X': X, 'local_pattern': local, 'long_range_pattern': longr, 'W': W, 'V': V, 'enc_bn_gamma': jnp.ones((F,), jnp.float32), 'enc_bn_beta': jnp.zeros((F,), jnp.float32), 'enc_mlp_W': jax.random.normal(ks[5], (F, F), dtype=jnp.float32) * 0.02, 'enc_mlp_b': jnp.zeros((F,), jnp.float32), 'enc_mlp_bn_gamma': jnp.ones((F,), jnp.float32), 'enc_mlp_bn_beta': jnp.zeros((F,), jnp.float32), 'dec_mlp_W': jax.random.normal(ks[6], (F, F), dtype=jnp.float32) * 0.02, 'dec_mlp_b': jnp.zeros((F,), jnp.float32), 'dec_mlp_bn_gamma': jnp.ones((F,), jnp.float32), 'dec_mlp_bn_beta': jnp.zeros((F,), jnp.float32)}
    _L0_gnn_all = _L0_gnn_setup()
    _L0_gnn_in = {k: v for k, v in _L0_gnn_all.items() if k in ('W', 'V', 'enc_bn_gamma', 'enc_bn_beta', 'enc_mlp_W', 'enc_mlp_b', 'enc_mlp_bn_gamma', 'enc_mlp_bn_beta', 'dec_mlp_W', 'dec_mlp_b', 'dec_mlp_bn_gamma', 'dec_mlp_bn_beta')}
    del _L0_gnn_all

    def _L1_gnn_setup():
        import jax, jax.numpy as jnp
        import numpy as np
        N = 4096
        IN_F = 256
        OUT_F = 256
        N_NEI = 4
        key = jax.random.key(seed)
        kx, ka, kw = jax.random.split(key, 3)
        x = jax.random.normal(kx, (N, IN_F), dtype=jnp.float32)
        adj_norm = jax.random.normal(ka, (N, N), dtype=jnp.float32) / jnp.sqrt(N).astype(jnp.float32)
        kaiming_std = np.sqrt(2.0 / IN_F).astype(np.float32)
        weight = jax.random.normal(kw, (N_NEI, IN_F, OUT_F), dtype=jnp.float32) * kaiming_std
        return {'x': x, 'adj_norm': adj_norm, 'weight': weight}
    _L1_gnn_all = _L1_gnn_setup()
    _L1_gnn_in = {k: v for k, v in _L1_gnn_all.items() if k in ('weight',)}
    del _L1_gnn_all
    return {'x': x, 'adj': adj, 'L0_gnn_W': _L0_gnn_in['W'], 'L0_gnn_V': _L0_gnn_in['V'], 'L0_gnn_enc_bn_gamma': _L0_gnn_in['enc_bn_gamma'], 'L0_gnn_enc_bn_beta': _L0_gnn_in['enc_bn_beta'], 'L0_gnn_enc_mlp_W': _L0_gnn_in['enc_mlp_W'], 'L0_gnn_enc_mlp_b': _L0_gnn_in['enc_mlp_b'], 'L0_gnn_enc_mlp_bn_gamma': _L0_gnn_in['enc_mlp_bn_gamma'], 'L0_gnn_enc_mlp_bn_beta': _L0_gnn_in['enc_mlp_bn_beta'], 'L0_gnn_dec_mlp_W': _L0_gnn_in['dec_mlp_W'], 'L0_gnn_dec_mlp_b': _L0_gnn_in['dec_mlp_b'], 'L0_gnn_dec_mlp_bn_gamma': _L0_gnn_in['dec_mlp_bn_gamma'], 'L0_gnn_dec_mlp_bn_beta': _L0_gnn_in['dec_mlp_bn_beta'], 'L1_gnn_weight': _L1_gnn_in['weight']}

def reference(x, adj, L0_gnn_W, L0_gnn_V, L0_gnn_enc_bn_gamma, L0_gnn_enc_bn_beta, L0_gnn_enc_mlp_W, L0_gnn_enc_mlp_b, L0_gnn_enc_mlp_bn_gamma, L0_gnn_enc_mlp_bn_beta, L0_gnn_dec_mlp_W, L0_gnn_dec_mlp_b, L0_gnn_dec_mlp_bn_gamma, L0_gnn_dec_mlp_bn_beta, L1_gnn_weight):
    import jax
    import jax.numpy as jnp

    def _L0_gnn_ref(X, local_pattern, long_range_pattern, W, V, enc_bn_gamma, enc_bn_beta, enc_mlp_W, enc_mlp_b, enc_mlp_bn_gamma, enc_mlp_bn_beta, dec_mlp_W, dec_mlp_b, dec_mlp_bn_gamma, dec_mlp_bn_beta):
        import jax, jax.numpy as jnp
        import numpy as np
        N, F, H = (1536, 256, 4)
        D = F // H
        ALPHA = 0.5
        EPS = 1e-06

        def _batchnorm(x, gamma, beta):
            m = jnp.mean(x, axis=0)
            v = jnp.var(x, axis=0)
            return (x - m) * jax.lax.rsqrt(v + EPS) * gamma + beta

        def _masked_softmax(scores, mask):
            s = jnp.where(mask, scores, -jnp.inf)
            att = jax.nn.softmax(s, axis=-1)
            return jnp.where(mask, att, 0.0)

        def _mlp_block(x, Wm, bm, g, b):
            h = jax.nn.elu(x @ Wm.T + bm) + x
            return _batchnorm(h, g, b)
        n = X.shape[0]
        Xh = X.reshape(n, H, D).transpose(1, 0, 2)
        Xw = jnp.einsum('hnd,hde->hne', Xh, W)
        f1 = jnp.einsum('hnd,hd->hn', Xw, V[:, 0, :, 0])
        f2 = jnp.einsum('hnd,hd->hn', Xw, V[:, 1, :, 0])
        sig = jax.nn.sigmoid(f1[:, :, None] + f2[:, None, :])
        lmask = (local_pattern != 0)[None]
        gmask = (long_range_pattern != 0)[None]
        local_att = _masked_softmax(local_pattern[None] * sig, lmask)
        long_att = _masked_softmax(long_range_pattern[None] * sig, gmask)
        att = ALPHA * long_att + (1.0 - ALPHA) * local_att
        Xa = jnp.einsum('hij,hjd->hid', att, Xw)
        Xc = Xa.transpose(1, 0, 2).reshape(n, F)
        Xn = _batchnorm(Xc, enc_bn_gamma, enc_bn_beta)
        emb = _mlp_block(Xn, enc_mlp_W, enc_mlp_b, enc_mlp_bn_gamma, enc_mlp_bn_beta)
        Yh = emb.reshape(n, H, D).transpose(1, 0, 2)
        Y = jnp.einsum('hij,hjd->hid', att, Yh)
        Y = jnp.einsum('hnd,hed->hne', Y, W)
        Yc = Y.transpose(1, 0, 2).reshape(n, F)
        Yc = jax.nn.elu(Yc)
        out = _mlp_block(Yc, dec_mlp_W, dec_mlp_b, dec_mlp_bn_gamma, dec_mlp_bn_beta)
        return out

    def _L1_gnn_ref(x, adj_norm, weight):
        import jax, jax.numpy as jnp
        import numpy as np
        N = 4096
        IN_F = 256
        OUT_F = 256
        N_NEI = 4
        out = x @ weight[0]
        p = x
        for idx in range(1, N_NEI):
            p = adj_norm @ p
            out = out + p @ weight[idx]
        return out
    x = _layernorm(x + _L0_gnn_ref(x, adj, adj, L0_gnn_W, L0_gnn_V, L0_gnn_enc_bn_gamma, L0_gnn_enc_bn_beta, L0_gnn_enc_mlp_W, L0_gnn_enc_mlp_b, L0_gnn_enc_mlp_bn_gamma, L0_gnn_enc_mlp_bn_beta, L0_gnn_dec_mlp_W, L0_gnn_dec_mlp_b, L0_gnn_dec_mlp_bn_gamma, L0_gnn_dec_mlp_bn_beta), axis=-1)
    x = _layernorm(x + _L1_gnn_ref(x, adj, L1_gnn_weight), axis=-1)
    return x

_drawn_inputs = setup_inputs


def setup_inputs(seed=0):
    import zlib

    import numpy as np

    out = dict(_drawn_inputs(seed))
    spreads = {'L0_gnn_enc_bn_gamma': (1.0, 0.2),
     'L0_gnn_enc_bn_beta': (0.0, 2.0),
     'L0_gnn_enc_mlp_b': (0.0, 0.8),
     'L0_gnn_enc_mlp_bn_gamma': (1.0, 0.2),
     'L0_gnn_enc_mlp_bn_beta': (0.0, 0.496),
     'L0_gnn_dec_mlp_b': (0.0, 0.753),
     'L0_gnn_dec_mlp_bn_gamma': (1.0, 0.2),
     'L0_gnn_dec_mlp_bn_beta': (0.0, 0.1)}
    factors = {}
    for name, (base, spread) in spreads.items():
        noise = np.random.default_rng([zlib.crc32(name.encode()), seed]).standard_normal(out[name].shape)
        drawn = base * np.exp(spread * noise) if base else spread * noise
        out[name] = jnp.asarray(drawn.astype(out[name].dtype))
    for name, factor in factors.items():
        out[name] = (out[name] * factor).astype(out[name].dtype)
    return out
```

```python
from contextlib import ExitStack

import concourse.bass as bass
from concourse import mybir
from concourse.alu_op_type import AluOpType as ALU

ACT = mybir.ActivationFunctionType
F32 = mybir.dt.float32
F32R = mybir.dt.float32r
U8 = mybir.dt.uint8
ds = bass.ds

P = 128
N = 4096
F = 256
H = 4
D = F // H
PAIRS = F // P
NT = N // P
SPAN = 2048
HALVES = N // SPAN
BLOCKS = HALVES * PAIRS
BANK = 512
STEPS = 4
ITERS = NT // STEPS
APP = BLOCKS * ITERS
CHUNK = 512
CHUNKS = N // CHUNK
CT = CHUNK // P
HOPS = 3
START = 1
SETUP_LOADS = 16 * 6
QUARTERS = SPAN // BANK
BN_EPS = 1e-6
LN_EPS = 1e-5
PARAMS = ["enc_g", "enc_b", "enc_mlp_b", "enc_mlp_g", "enc_mlp_beta", "dec_mlp_b", "dec_mlp_g", "dec_mlp_beta"]


def gnn_kernel(nc, x, xT, adjT, head_w, head_wT, v1, v2_row, params, enc_wT, dec_wT, hop_w, out):
    f1_dram = nc.dram_tensor("f1_scratch", [H, N], F32, kind="Internal").ap()
    adj8_dram = nc.dram_tensor("adj8_scratch", [((CHUNKS + 1) * ITERS * P * STEPS), BANK], U8, kind="Internal").ap()
    scores_dram = nc.dram_tensor("scores_scratch", [APP, 2, P, 2 * SPAN], F32, kind="Internal").ap()
    inv_dram = nc.dram_tensor("inv_scratch", [BLOCKS, P, SPAN], F32, kind="Internal").ap()
    xw_dram = nc.dram_tensor("xw_scratch", [NT, P, HOPS, F], F32, kind="Internal").ap()

    base = nc.sbuf_base + (-nc.sbuf_base) % 64
    end = nc.sbuf_usable_end

    def placer(at):
        def place(name, shape, dt=F32, size=4):
            n = size
            for s in shape[1:]:
                n *= s
            assert place.at + n <= end, (name, place.at + n - end)
            t = nc.alloc_sbuf_tensor_at(name, shape, dt, offset=place.at)
            place.at += n + (-n) % 32
            return t
        place.at = at
        return place

    const = placer(base)
    w_sb = const("w_sb", [P, PAIRS, P])
    wT_sb = const("wT_sb", [P, PAIRS, P])
    v_sb = const("v_sb", [P, PAIRS])
    wv = const("wv", [P, PAIRS])
    wv_cols = const("wv_cols", [P, PAIRS, P])
    par = const("par", [P, len(PARAMS), PAIRS])
    encw = const("encw", [P, PAIRS, F])
    decw = const("decw", [P, PAIRS, F])
    ident = const("ident", [P, P])
    ones = const("ones", [P, 32])
    minus_half = const("minus_half", [P, CT])
    spread = const("spread", [P, 2, P])
    f2_half = const("f2_half", [P, NT, H])
    stats = const("stats", [P, PAIRS, CHUNKS, 6])
    moments = const("moments", [P, PAIRS, 2])
    norm = const("norm", [P, 4, PAIRS])
    ln_stats = const("ln_stats", [P, CT, 6])
    ln_mom = const("ln_mom", [P, CT, 2])
    ln_small = const("ln_small", [P, 3, CT])
    ln_gate = const("ln_gate", [P, 1])
    region = const.at

    att = placer(region)
    hT = att("hT", [P, PAIRS, N])
    values = att("values", [P, NT, F])
    f1_rows = att("f1_rows", [P, PAIRS, 2, SPAN])
    ring = att("ring", [P, STEPS, 2, SPAN])
    inv_den = att("inv_den", [P, 2 * BANK])
    inv_blk = att("inv_blk", [P, SPAN])
    mask_at = att.at
    mask = att("mask", [P, 2, SPAN])
    mask8 = att("mask8", [P, 2, SPAN], U8, 1)
    lhs = att("lhs", [P, STEPS, P])

    mid = placer(region + 4 * (PAIRS * N + NT * F + 2 * SPAN))
    cin = mid("cin", [P, 2, PAIRS, CHUNK])
    mid = placer(mask_at)
    cexp = mid("cexp", [P, 2, PAIRS, CHUNK])
    crelu = mid("crelu", [P, 2, PAIRS, CHUNK])
    early = placer(region + 4 * (PAIRS * N + NT * F + PAIRS * 2 * SPAN))
    v2_b = early("v2_b", [P, F])
    f1_stage = early("f1_stage", [P, 2, CHUNK])
    prod = early("prod", [P, 2, CT, F])

    hop = placer(region)
    q1 = hop("q1", [P, NT, 2, F], F32R)
    q0 = hop("q0", [P, NT, 2, F], F32R)
    x2 = hop("x2", [P, NT, F])
    tail = hop.at
    adj8 = hop("adj8", [P, 2, STEPS * BANK], U8, 1)
    adjr = hop("adjr", [P, 2, STEPS, BANK], F32R)
    xw = hop("xw", [P, 2, CT, F])
    total = hop("total", [P, CT, F])

    ln = placer(region + 4 * PAIRS * N)
    hopw = ln("hopw", [P, PAIRS, 4 * F])
    xin = ln("xin", [P, 2, CT, F])
    product3 = ln("product3", [P, CT, F])
    lt = placer(tail)
    normed = lt("normed", [P, 2, PAIRS, CHUNK])
    y = lt("y", [P, 2, CT, F])
    x2T = lt("x2T", [P, 2, PAIRS, CHUNK])
    products = [ln("products0", [P, CT, HOPS * F]), lt("products1", [P, CT, HOPS * F])]

    ctx = ExitStack()
    with ctx:
        psA = ctx.enter_context(nc.psum_tensor("psA", [P, 4 * BANK], F32))
        psB = ctx.enter_context(nc.psum_tensor("psB", [P, 4 * BANK], F32))

        def sem(name):
            return ctx.enter_context(nc.semaphore(name))

        def slots(name, n=2):
            return [sem(f"{name}{i}") for i in range(n)]

        weights_zeroed = sem("weights_zeroed")
        started = sem("started")
        weights_in = sem("weights_in")
        consts_set = sem("consts_set")
        ident0 = sem("ident0")
        ident_set = sem("ident_set")
        wv_mm = sem("wv_mm")
        wv_ready = sem("wv_ready")
        set_in = slots("set_in")
        set_mm = slots("set_mm")
        f1_mm = slots("f1_mm")
        set_copied = slots("set_copied")
        f1_staged = slots("f1_staged")
        f1_stored = slots("f1_stored")
        f2_prod = slots("f2_prod")
        f2_sum = slots("f2_sum")
        f2_ready = sem("f2_ready")
        f1_in = slots("f1_in")
        adj_in = slots("adj_in", STEPS)
        adj8_ready = slots("adj8_ready", STEPS)
        adj8_out = slots("adj8_out", STEPS)
        tanh_done = slots("tanh_done", STEPS)
        exp_done = slots("exp_done", STEPS)
        masked = slots("masked", STEPS)
        lhs_ready = slots("lhs_ready", STEPS)
        contracted = slots("contracted", STEPS)
        spilled = slots("spilled", STEPS)
        scores_in = slots("scores_in", STEPS)
        mask_in = slots("mask_in", STEPS)
        sums_copied = sem("sums_copied")
        evacuated = sem("evacuated")
        inv_ready = sem("inv_ready")
        spread_done = sem("spread_done")
        inv_copied = sem("inv_copied")
        inv_stored = sem("inv_stored")
        inv_in = sem("inv_in")
        scaled = sem("scaled")
        elu_exp = sem("elu_exp")
        elu_min = sem("elu_min")
        elu_done = sem("elu_done")
        chunk = {}
        for tag, names in (("enc", ("cin", "mm", "act", "mixed", "h")), ("emb", ("cin", "mm", "act")),
                           ("dec", ("mm", "act", "mixed", "h"))):
            chunk[tag] = {n: slots(f"{tag}_{n}") for n in names}
        stats_done = sem("stats_done")
        var_ready = sem("var_ready")
        rstd_ready = sem("rstd_ready")
        dve_small = sem("dve_small")
        hopw_in = sem("hopw_in")
        x_in = slots("x_in")
        normed_ready = slots("normed_ready")
        turned = slots("turned")
        summed = slots("summed")
        ln_var = sem("ln_var")
        ln_rstd = sem("ln_rstd")
        ln_small_done = sem("ln_small_done")
        x2_ready = slots("x2_ready")
        x2_turned = slots("x2_turned")
        x2T_ready = slots("x2T_ready")
        x2_kept = slots("x2_kept")
        prod_mm = sem("prod_mm")
        prod_copied = sem("prod_copied")
        prod_stored = sem("prod_stored")
        prod_free = slots("prod_free")
        q_hi = sem("q_hi")
        q_lo = sem("q_lo")
        hop_adj_in = slots("hop_adj_in")
        cast_done = slots("cast_done")
        hop_contracted = slots("hop_contracted")
        xw_in = slots("xw_in")
        hop_evac = slots("hop_evac")
        sum1 = sem("sum1")
        sum2 = sem("sum2")
        hop_hi = sem("hop_hi")
        hop_q = sem("hop_q")
        out_ready = sem("out_ready")
        out_stored = sem("out_stored")
        out_free = sem("out_free")

        reused = [set_mm, set_copied, f1_staged, f1_stored, f2_sum, contracted, adj8_out, spilled, summed,
                  turned, x2_turned, x2_kept, x2T_ready, hop_evac, cast_done, hop_contracted]
        reused = [s for group in reused for s in group]
        reused += [*prod_free, q_lo, prod_copied, out_free]
        reused += [s for tag in chunk for n in ("act", "mm", "h") if n in chunk[tag] for s in chunk[tag][n]]

        block = ctx.enter_context(nc.Block())

        xT_view = xT.rearrange("(q p) n -> p q n", p=P)
        x_view = x.rearrange("(c t p) f -> c p t f", t=CT, p=P)
        out_view = out.rearrange("(c t p) f -> c p t f", t=CT, p=P)

        den = psB[:, 0:2 * BANK]
        spread_ps = psB[:, 2 * BANK:4 * BANK]
        chunk_ps = [psA[:, s * 2 * BANK:(s + 1) * 2 * BANK] for s in range(2)]

        @block.sync
        def _(sp):
            sp.dma_start(v_sb[:], v1).then_inc(weights_in, 16)
            sp.wait_ge(weights_zeroed, 2)
            for dst, src in ((wT_sb, head_wT), (w_sb, head_w)):
                for hh in range(2):
                    a = slice(D * hh, D * (hh + 1))
                    sp.dma_start(dst[a, :, a], src[a]).then_inc(weights_in, 16)
            sp.dma_start(v2_b[:], v2_row.partition_broadcast(P)).then_inc(weights_in, 16)
            sp.wait_ge(started, 1)
            with sp.Fori(0, CHUNKS // 2) as i:
                for c in range(2):
                    sp.wait_ge(set_mm[c], i + START)
                    sp.dma_start(cin[:, c], xT_view[:, :, ds((2 * i + c) * CHUNK, CHUNK)]).then_inc(set_in[c], 16)

            def adj8_step(half, j, t):
                span = QUARTERS * ITERS * P * STEPS
                return adj8_dram[ds(half * span + j * (P * STEPS) + t + 1, span)].rearrange(
                    "(h p y) x -> p h y x", h=QUARTERS, y=STEPS)[0:P, :, 0]

            def load_adj(half, j, t, slot):
                sp.dma_start(mask[:, slot], adjT[ds(half * NT + j * STEPS + t, 1)].rearrange("a p x -> p (a x)")
                             ).then_inc(adj_in[t % STEPS], 16)

            def load_mask(at, t, slot):
                sp.dma_start(mask8[:, slot].rearrange("p (h x) -> p h x", h=QUARTERS), at).then_inc(mask_in[t], 16)

            def spill(it, t):
                sp.dma_start(scores_dram[ds(it, 1), t // 2].rearrange("a p x -> p (a x)"),
                             ring[:, t].rearrange("p h i -> p (h i)")).then_inc(spilled[t], 16)

            def read_adjacency(b, j, last):
                half, it = b // PAIRS, b * ITERS + j
                for t in range(STEPS):
                    sp.wait_ge(adj8_ready[t], half * ITERS + j + 1)
                    if t < 2:
                        load_adj(half, j, t + 2, t)
                    elif not last:
                        sp.dma_start(mask[:, t - 2], adjT[ds(half * NT + j * STEPS + t + 2, 1)].rearrange(
                            "a p x -> p (a x)")).then_inc(adj_in[t - 2], 16)
                    sp.dma_start(adj8_step(half, j, t), mask8[:, t % 2].rearrange("p (h x) -> p h x", h=QUARTERS)
                                 ).then_inc(adj8_out[t], 16)
                    if t % 2 == 0 and (t or not isinstance(j, int) or j):
                        before = (it, t - 1) if t else (it - 1, STEPS - 1)
                        sp.wait_ge(masked[before[1]], 2 * before[0] + 2)
                        spill(*before)
                    if last and t > 1:
                        sp.wait_ge(adj8_out[t - 2], 16 * (half + 1) * ITERS + START)
                        sp.wait_ge(adj8_out[t], 16 * (half + 1) * ITERS + START)
                        sp.wait_ge(masked[t], 2 * it + 2)
                        load_mask(adj8_step(half, 0, t - 2), t - 2, t - 2)
                if last:
                    spill(it, STEPS - 1)

            def read_masks(b, j, last):
                half, it = b // PAIRS, b * ITERS + j
                for t in range(STEPS):
                    ahead = t + 2 - STEPS * (t >= 2)
                    load = t < 2 or not last
                    at = adj8_step(half, j + (t >= 2), ahead) if load else None
                    sp.wait_ge(masked[t], 2 * it + 2)
                    if load:
                        load_mask(at, ahead, t % 2)
                    if t % 2:
                        spill(it, t)

            def store_inv(b):
                sp.wait_ge(inv_copied, 2 * b + 2)
                sp.dma_start(inv_dram[b], inv_blk[:]).then_inc(inv_stored, 16)

            for t in range(2):
                load_adj(0, 0, t, t)
            sp.dma_start(par[:], params).then_inc(weights_in, 16)
            sp.dma_start(encw[:], enc_wT).then_inc(weights_in, 16)
            sp.dma_start(decw[:], dec_wT).then_inc(weights_in, 16)
            for b in range(BLOCKS):
                half = b // PAIRS
                body = read_masks if b % PAIRS else read_adjacency
                if b % PAIRS and b + 1 < BLOCKS:
                    for t in range(2):
                        load_adj(half + 1, 0, t, t)
                body(b, 0, False)
                with sp.Fori(1, ITERS - 1) as j:
                    body(b, j, False)
                if b:
                    store_inv(b - 1)
                body(b, ITERS - 1, True)
            store_inv(BLOCKS - 1)

            def second(b, j):
                half, it = b // PAIRS, b * ITERS + j
                for t in range(STEPS):
                    if t % 2:
                        sp.wait_ge(contracted[t], APP + it + START)
                        sp.dma_start(ring[:, t].rearrange("p h i -> p (h i)"),
                                     scores_dram[ds(it, 1), t // 2].rearrange("a p x -> p (a x)")
                                     ).then_inc(scores_in[t], 16)
                    else:
                        at = adj8_step(half, j, t)
                        sp.wait_ge(masked[t], 2 * (APP + it))
                        load_mask(at, t, t // 2)

            for t in (1, 3):
                sp.wait_ge(spilled[t], 16 * APP + START)
                sp.wait_ge(masked[t], 2 * APP)
            for b in range(BLOCKS):
                with sp.Fori(0, ITERS - 1) as j:
                    second(b, j)
                sp.wait_ge(inv_stored, 16 * BLOCKS)
                if b:
                    sp.wait_ge(elu_done, b)
                sp.dma_start(inv_blk[:], inv_dram[b]).then_inc(inv_in, 16)
                second(b, ITERS - 1)

            sp.wait_ge(contracted[STEPS - 1], 2 * APP + START)
            sp.dma_start(hopw[:].rearrange("p q (k f) -> p q k f", k=4), hop_w).then_inc(hopw_in, 16)
            with sp.Fori(0, CHUNKS // 2) as i:
                for c in range(2):
                    sp.wait_ge(summed[c], i + START)
                    sp.dma_start(xin[:, c], x_view[ds(2 * i + c, 1)].rearrange("a p t f -> p (a t) f")
                                 ).then_inc(x_in[c], 16)

            sp.wait_ge(x2_kept[1], CHUNKS // 2 + START)
            sp.wait_ge(prod_mm, CHUNKS * CT)
            for c in range(2):
                sp.wait_ge(prod_free[c], CHUNKS // 2 + START)
            for n in range(HOPS):
                with sp.Fori(0, BLOCKS) as ib:
                    for c in range(2):
                        sp.wait_ge(hop_evac[c], n * BLOCKS + ib + START)
                        sp.dma_start(xw[:, c], xw_dram[ds((2 * ib + c) * CT, CT), :, HOPS - 1 - n].rearrange("t p f -> p t f")
                                     ).then_inc(xw_in[c], 16)
                        with sp.Fori(0, ITERS // 2) as jp:
                            for s in range(2):
                                sp.wait_ge(cast_done[s], n * APP + ib * ITERS + c * (ITERS // 2) + jp + START)
                                sp.dma_start(adj8[:, s], adj8_dram[
                                    ds(((2 * ib + c) * ITERS + 2 * jp + s) * (P * STEPS) + 1, P * STEPS)].rearrange(
                                        "(p t) x -> p (t x)", p=P)).then_inc(hop_adj_in[s], 16)

        @block.tensor
        def _(pe):
            def head_products(i, c, w, copied, done):
                pe.wait_ge(copied[c], i + START)
                for t in range(CT):
                    for q in range(PAIRS):
                        at = t * F + q * P
                        mm = pe.matmul(chunk_ps[c][:, at:at + P], cin[:, c, q, t * P:(t + 1) * P], w[:, q, :],
                                       start=True, stop=True)
                mm.then_inc(done[c], 1)

            pe.wait_ge(started, 1)
            pe.wait_ge(weights_in, SETUP_LOADS)
            for q in range(PAIRS):
                mm = pe.matmul(psB[:, q:q + 1], wT_sb[:, q, :], v_sb[:, q:q + 1], start=True, stop=True)
            mm.then_inc(wv_mm, 1)
            pe.wait_ge(wv_ready, 1)
            with pe.Fori(0, CHUNKS // 2) as i:
                for c in range(2):
                    pe.wait_ge(set_in[c], 16 * (i + 1))
                    pe.wait_ge(f1_staged[c], i + START)
                    for q in range(PAIRS):
                        mm = pe.matmul(psB[:, c * BANK:(c + 1) * BANK], wv_cols[:, q, :], cin[:, c, q, :],
                                       start=q == 0, stop=q == PAIRS - 1)
                    mm.then_inc(f1_mm[c], 1)
                    head_products(i, c, w_sb, set_copied, set_mm)

            def step(use, t, a, acc, first, last):
                pe.wait_ge(lhs_ready[t], use + 1)
                if a == 1 and t % 2:
                    pe.wait_ge(scores_in[t], 16 * (use - APP + 1))
                else:
                    pe.wait_ge(masked[t], 2 * use + 2)
                for k in range(QUARTERS):
                    at = slice(k * BANK, (k + 1) * BANK)
                    for hh in range(2):
                        mm = pe.matmul(acc[D * hh:D * hh + D, at], lhs[:, t, hh * D:(hh + 1) * D], ring[:, t, hh, at],
                                       start=first, stop=last, tile_position=(0, D * hh))
                if a == 0:
                    for k in range(QUARTERS):
                        for hh in range(2):
                            g = 32 * (2 * hh + k % 2)
                            mm = pe.matmul(den[g:g + 32, k // 2 * BANK:(k // 2 + 1) * BANK], ones[:],
                                           ring[:, t, hh, k * BANK:(k + 1) * BANK],
                                           start=first, stop=last, tile_position=(0, g))
                mm.then_inc(contracted[t], 1)

            def spread_inv(b):
                for r in range(2):
                    pe.wait_ge(inv_ready, 2 * b + r + 1)
                    if 2 * b + r:
                        pe.wait_ge(inv_copied, 2 * b + r)
                    for k in range(2):
                        mm = pe.matmul(spread_ps[:, k * BANK:(k + 1) * BANK], spread[:, k, :],
                                       inv_den[:, r * BANK:(r + 1) * BANK], start=True, stop=True)
                    mm.then_inc(spread_done, 1)

            def application(a):
                for b in range(BLOCKS):
                    acc = (psA, psB)[b % 2] if a else psA
                    if a == 0 and b:
                        pe.wait_ge(evacuated, b)
                    elif b >= 2:
                        pe.wait_ge(evacuated, BLOCKS + b - 1)
                    use = a * APP + b * ITERS
                    for t in range(STEPS):
                        step(use, t, a, acc, t == 0, False)
                    if a == 0 and b:
                        spread_inv(b - 1)
                    with pe.Fori(1, ITERS - 1) as j:
                        for t in range(STEPS):
                            step(use + j, t, a, acc, False, False)
                    for t in range(STEPS):
                        step(use + ITERS - 1, t, a, acc, False, t == STEPS - 1)
                if a == 0:
                    spread_inv(BLOCKS - 1)

            def mlp(tag, w):
                s = chunk[tag]
                with pe.Fori(0, CHUNKS // 2) as i:
                    for c in range(2):
                        if tag == "enc":
                            pe.wait_ge(s["cin"][c], i + 1)
                        pe.wait_ge(s["act"][c], i + START)
                        for o in range(PAIRS):
                            for q in range(PAIRS):
                                mm = pe.matmul(chunk_ps[c][:, o * BANK:(o + 1) * BANK], w[:, q, o * P:(o + 1) * P],
                                               hT[:, q, ds((2 * i + c) * CHUNK, CHUNK)],
                                               start=q == 0, stop=q == PAIRS - 1)
                        mm.then_inc(s["mm"][c], 1)

            application(0)
            pe.wait_ge(weights_in, SETUP_LOADS + 3 * 16)
            pe.wait_ge(evacuated, BLOCKS)
            mlp("enc", encw)
            with pe.Fori(0, CHUNKS // 2) as i:
                for c in range(2):
                    pe.wait_ge(chunk["emb"]["cin"][c], i + 1)
                    head_products(i, c, wT_sb, chunk["emb"]["act"], chunk["emb"]["mm"])
            application(1)
            pe.wait_ge(elu_done, BLOCKS)
            mlp("dec", decw)

            def turn(i, c):
                pe.wait_ge(normed_ready[c], i + 1)
                if c:
                    pe.wait_ge(summed[0], i + 1 + START)
                else:
                    pe.wait_ge(summed[1], i + START)
                for t in range(CT):
                    for q in range(PAIRS):
                        at = t * F + q * P
                        mm = pe.transpose(psA[:, at:at + P], normed[:, c, q, t * P:(t + 1) * P], ident[:])
                mm.then_inc(turned[c], 1)

            def turn_x2(i, c):
                pe.wait_ge(x2_ready[c], i + 1)
                if c:
                    pe.wait_ge(x2T_ready[0], i + 1 + START)
                else:
                    pe.wait_ge(x2T_ready[1], i + START)
                for t in range(CT):
                    for q in range(PAIRS):
                        at = 2 * BANK + q * CHUNK + t * P
                        mm = pe.transpose(psA[:, at:at + P], y[:, c, t, q * P:(q + 1) * P], ident[:])
                mm.then_inc(x2_turned[c], 1)

            def hop_products(i, c):
                pe.wait_ge(x2T_ready[c], i + 1 + START)
                for t in range(CT):
                    before = 2 * i * CT + c * CT + t
                    pe.wait_ge(prod_copied, (before - 1 if c or t >= 2 else 2 * i * CT) + START)
                    for half in range(2):
                        for q in range(PAIRS):
                            mm = pe.matmul(psB[:, (2 * (t % 2) + half) * BANK:(2 * (t % 2) + half + 1) * BANK],
                                           x2T[:, c, q, t * P:(t + 1) * P], hopw[:, q, half * BANK:(half + 1) * BANK],
                                           start=q == 0, stop=q == PAIRS - 1)
                    mm.then_inc(prod_mm, 1)

            pe.wait_ge(hopw_in, 16)
            pe.wait_ge(ident_set, 1)
            turn(0, 0)
            with pe.Fori(0, CHUNKS // 2 - 1) as i:
                turn_x2(i, 0)
                turn(i, 1)
                hop_products(i, 0)
                turn_x2(i, 1)
                turn(i + 1, 0)
                hop_products(i, 1)
            i = CHUNKS // 2 - 1
            turn_x2(i, 0)
            turn(i, 1)
            hop_products(i, 0)
            turn_x2(i, 1)
            hop_products(i, 1)

            def contract(n, ib, c, jp, s, first, last):
                src = (q0, q1)[n % 2]
                acc = (psA, psB)[c]
                use = n * APP + ib * ITERS + c * (ITERS // 2) + jp
                pe.wait_ge(cast_done[s], use + 1 + START)
                for t in range(STEPS):
                    j = (2 * jp + s) * STEPS + t
                    for m in range(CT):
                        mm = pe.matmul(acc[:, m * BANK:(m + 1) * BANK], adjr[:, s, t, m * P:(m + 1) * P],
                                       src[:, ds(j, 1)].rearrange("p a k f -> p (a k f)"),
                                       start=first and t == 0, stop=last and t == STEPS - 1)
                mm.then_inc(hop_contracted[s], 1)

            pe.wait_ge(q_lo, CHUNKS + START)
            pe.wait_ge(q_hi, CHUNKS)
            for n in range(HOPS):
                if n:
                    pe.wait_ge(hop_q, 2 * BLOCKS * n)
                with pe.Fori(0, BLOCKS) as ib:
                    for c in range(2):
                        pe.wait_ge(hop_evac[c], n * BLOCKS + ib + START)
                        contract(n, ib, c, 0, 0, True, False)
                        contract(n, ib, c, 0, 1, False, False)
                        with pe.Fori(1, ITERS // 2 - 1) as jp:
                            contract(n, ib, c, jp, 0, False, False)
                            contract(n, ib, c, jp, 1, False, False)
                        contract(n, ib, c, ITERS // 2 - 1, 0, False, False)
                        contract(n, ib, c, ITERS // 2 - 1, 1, False, True)

        @block.scalar
        def _(act):
            def copy_values(i, c, mm, done):
                act.wait_ge(mm[c], i + 1 + START)
                act.activation(values[:, ds((2 * i + c) * CT, CT), :].rearrange("p t f -> p (t f)"), chunk_ps[c],
                               ACT.Copy).then_inc(done[c], 1)

            act.wait_ge(started, 1)
            with act.Fori(0, CHUNKS // 2) as i:
                for c in range(2):
                    act.wait_ge(f1_mm[c], i + 1)
                    act.wait_ge(f1_stored[c], 16 * i + START)
                    act.activation(f1_stage[:, c], psB[:, c * BANK:(c + 1) * BANK], ACT.Copy).then_inc(f1_staged[c], 1)
                    copy_values(i, c, set_mm, set_copied)
                    act.wait_ge(f1_staged[c], i + 1 + START)
                    act.dma_start(f1_dram[:, ds((2 * i + c) * CHUNK, CHUNK)],
                                  f1_stage[0:P:P // H, c]).then_inc(f1_stored[c], 16)

            def load_f1(b):
                half, q = b // PAIRS, b % PAIRS
                for hh in range(2):
                    act.dma_start(f1_rows[:, q, hh], f1_dram[2 * q + hh, half * SPAN:(half + 1) * SPAN]
                                  .partition_broadcast(P)).then_inc(f1_in[hh], 16)

            for c in range(2):
                act.wait_ge(f1_stored[c], 16 * CHUNKS // 2 + START)
            load_f1(0)

            def scores(a, b, j, t):
                q, it = b % PAIRS, b * ITERS + j
                use = a * APP + it
                act.wait_ge(contracted[t], use + START)
                if t % 2:
                    act.wait_ge(spilled[t], 16 * it + START)
                for hh in range(2):
                    if isinstance(j, int):
                        act.wait_ge(f1_in[hh], 16 * (a * BLOCKS + b + 1))
                    act.activation(ring[:, t, hh], f1_rows[:, q, hh], ACT.Tanh,
                                   bias=f2_half[:, ds(j * STEPS + t, 1), 2 * q + hh], scale=0.5).then_inc(tanh_done[t], 1)
                if a == 0:
                    both = ring[:, t].rearrange("p h i -> p (h i)")
                    act.wait_ge(tanh_done[t], 2 * use + 2)
                    act.activation(both, both, ACT.Exp, scale=0.5).then_inc(exp_done[t], 1)
                else:
                    for hh in range(2):
                        act.wait_ge(tanh_done[t], 2 * use + hh + 1)
                        act.activation(ring[:, t, hh], ring[:, t, hh], ACT.Exp, scale=0.5).then_inc(exp_done[t], 1)

            def mlp(tag, bias):
                s = chunk[tag]
                with act.Fori(0, CHUNKS // 2) as i:
                    for c in range(2):
                        act.wait_ge(s["mm"][c], i + 1 + START)
                        act.wait_ge(s["h"][c], i + START)
                        for o in range(PAIRS):
                            src = chunk_ps[c][:, o * BANK:(o + 1) * BANK]
                            act.activation(cexp[:, c, o], src, ACT.Exp, bias=par[:, bias, o:o + 1])
                            ins = act.activation(crelu[:, c, o], src, ACT.Relu, bias=par[:, bias, o:o + 1])
                        ins.then_inc(s["act"][c], 1)

            act.wait_ge(f2_ready, CHUNKS)
            for b in range(BLOCKS):
                for t in range(STEPS):
                    scores(0, b, 0, t)
                    if t == 1:
                        load_f1((b + 1) % BLOCKS)
                with act.Fori(1, ITERS) as j:
                    for t in range(STEPS):
                        scores(0, b, j, t)

            for t in (0, 2):
                scores(1, 0, 0, t)
            act.wait_ge(weights_in, SETUP_LOADS + 3 * 16)
            mlp("enc", PARAMS.index("enc_mlp_b"))
            with act.Fori(0, CHUNKS // 2) as i:
                for c in range(2):
                    copy_values(i, c, chunk["emb"]["mm"], chunk["emb"]["act"])

            def elu_exps(b):
                half, q = b // PAIRS, b % PAIRS
                act.wait_ge(evacuated, BLOCKS + b + 1)
                act.activation(inv_blk[:], hT[:, q, half * SPAN:(half + 1) * SPAN], ACT.Exp).then_inc(elu_exp, 1)

            for b in range(BLOCKS):
                if b:
                    for t in (0, 2):
                        scores(1, b, 0, t)
                    elu_exps(b - 1)
                if b + 1 < BLOCKS:
                    load_f1(b + 1)
                with act.Fori(1, ITERS) as j:
                    for t in (0, 2):
                        scores(1, b, j, t)
            elu_exps(BLOCKS - 1)
            mlp("dec", PARAMS.index("dec_mlp_b"))

            with act.Fori(0, CHUNKS // 2) as i:
                for c in range(2):
                    ch = 2 * i + c
                    act.wait_ge(x2_turned[c], i + 1 + START)
                    act.activation(x2T[:, c].rearrange("p q n -> p (q n)"), psA[:, 2 * BANK:4 * BANK], ACT.Copy
                                   ).then_inc(x2T_ready[c], 1)
                    act.activation(x2[:, ds(ch * CT, CT)], y[:, c], ACT.Copy).then_inc(x2_kept[c], 1)
                    act.wait_ge(prod_free[c], i + START)
                    act.wait_ge(q_lo, ch + START)
                    for t in range(CT):
                        src = psB[:, 2 * (t % 2) * BANK:2 * (t % 2 + 1) * BANK]
                        act.wait_ge(prod_mm, ch * CT + t + 1)
                        act.activation(products[c][:, t], src[:, 0:HOPS * F], ACT.Copy)
                        act.activation(product3[:, t], src[:, HOPS * F:], ACT.Copy).then_inc(prod_copied, 1)

            for n in range(HOPS):
                with act.Fori(0, APP) as u:
                    for s in range(2):
                        act.wait_ge(hop_adj_in[s], 16 * (n * APP + u + 1))
                        act.wait_ge(hop_contracted[s], n * APP + u + START)
                        act.activation(adjr[:, s].rearrange("p t x -> p (t x)"), adj8[:, s], ACT.Copy
                                       ).then_inc(cast_done[s], 1)

        @block.vector
        def _(dve):
            small = [0]

            def link(ins):
                small[0] += 1
                ins.then_inc(dve_small, 1)
                dve.wait_ge(dve_small, small[0])

            dve.memset(wT_sb[:], 0.0).then_inc(weights_zeroed, 1)
            dve.memset(w_sb[:], 0.0).then_inc(weights_zeroed, 1)
            dve.wait_ge(started, 1)
            dve.memset(ones[:], 1.0)
            dve.memset(minus_half[:], -0.5).then_inc(consts_set, 1)
            link(dve.memset(spread[:], 0.0))
            for k in range(2):
                for hh in range(2):
                    g = 32 * (2 * hh + k)
                    ins = dve.memset(spread[g:g + 1, k, D * hh:D * (hh + 1)], 1.0)
            link(ins)
            link(dve.memset(wv_cols[:], 0.0))
            dve.wait_ge(wv_mm, 1)
            link(dve.tensor_copy(wv[:], psB[:, 0:PAIRS]))
            for h in range(H):
                a = slice(D * (h % 2), D * (h % 2 + 1))
                ins = dve.tensor_scalar(wv_cols[a, h // 2, 32 * h:32 * h + 32], ones[a, :], wv[a, h // 2:h // 2 + 1], None,
                                        ALU.mult)
            ins.then_inc(wv_ready, 1)

            dve.wait_ge(weights_in, SETUP_LOADS)
            with dve.Fori(0, CHUNKS // 2) as i:
                for c in range(2):
                    here = ds((2 * i + c) * CT, CT)
                    dve.wait_ge(set_copied[c], i + 1 + START)
                    dve.wait_ge(f2_sum[c], i + START)
                    dve.tensor_tensor(prod[:, c], values[:, here, :], v2_b[:].unsqueeze(1).to_broadcast([P, CT, F]),
                                      ALU.mult).then_inc(f2_prod[c], 1)
                    dve.wait_ge(f2_prod[c], i + 1)
                    dve.tensor_reduce(f2_half[:, here, :], prod[:, c].rearrange("p t (h e) -> p t h e", h=H),
                                      mybir.AxisListType.X, ALU.add).then_inc(f2_sum[c], 1)
                    dve.wait_ge(f2_sum[c], i + 1 + START)
                    dve.tensor_scalar(f2_half[:, here, :], f2_half[:, here, :], 0.5, None, ALU.mult).then_inc(f2_ready, 1)

            def mask_scores(a, use, t, m):
                for hh in range(2):
                    if a == 0:
                        dve.wait_ge(exp_done[t], use + 1)
                    else:
                        dve.wait_ge(exp_done[t], APP + 2 * (use - APP) + hh + 1)
                    dve.tensor_tensor(ring[:, t, hh], ring[:, t, hh], m, ALU.mult).then_inc(masked[t], 1)

            def keep_lhs(use, t, j, q):
                dve.wait_ge(contracted[t], use + START)
                dve.tensor_copy(lhs[:, t:t + 1], values[:, ds(j * STEPS + t, 1), q * P:(q + 1) * P]
                                ).then_inc(lhs_ready[t], 1)

            def bn_coefficients(g, b):
                for q in range(PAIRS):
                    ins = dve.bn_aggr(moments[:, q], stats[:, q].rearrange("p c s -> p (c s)"))
                link(ins)
                dve.tensor_scalar(norm[:, 0], moments[:, :, 1], BN_EPS, None, ALU.add).then_inc(var_ready, 1)
                bn_coefficients.n += 1
                dve.wait_ge(rstd_ready, bn_coefficients.n)
                link(dve.tensor_tensor(norm[:, 2], norm[:, 1], par[:, g], ALU.mult))
                link(dve.tensor_tensor(norm[:, 0], moments[:, :, 0], norm[:, 2], ALU.mult))
                link(dve.tensor_tensor(norm[:, 3], par[:, b], norm[:, 0], ALU.subtract))
            bn_coefficients.n = 0

            def apply_bn(dst, ch, done):
                for q in range(PAIRS):
                    ins = dve.tensor_scalar(dst[:, q], hT[:, q, ds(ch * CHUNK, CHUNK)], norm[:, 2, q:q + 1],
                                            norm[:, 3, q:q + 1], ALU.mult, ALU.add)
                ins.then_inc(done, 1)

            def mlp(tag):
                s = chunk[tag]

                def prepare(ch, c):
                    if tag == "enc":
                        apply_bn(hT[:, :, ds(ch * CHUNK, CHUNK)], ch, s["cin"][c])

                def mix(i, c):
                    ch = 2 * i + c
                    here = hT[:, :, ds(ch * CHUNK, CHUNK)]
                    dve.wait_ge(s["act"][c], i + 1 + START)
                    dve.scalar_tensor_tensor(out=cexp[:, c], in0=cexp[:, c], scalar=1.0, in1=here,
                                             op0=ALU.min, op1=ALU.add).then_inc(s["mixed"][c], 1)
                    dve.wait_ge(s["mixed"][c], i + 1)
                    dve.scalar_tensor_tensor(out=here, in0=cexp[:, c], scalar=-1.0, in1=crelu[:, c],
                                             op0=ALU.add, op1=ALU.add).then_inc(s["h"][c], 1)
                    dve.wait_ge(s["h"][c], i + 1 + START)
                    for q in range(PAIRS):
                        ins = dve.bn_stats(stats[:, q, ds(ch, 1)].rearrange("p a s -> p (a s)"),
                                           hT[:, q, ds(ch * CHUNK, CHUNK)])
                    ins.then_inc(stats_done, 1)

                prepare(0, 0)
                prepare(1, 1)
                with dve.Fori(0, CHUNKS // 2 - 1) as i:
                    prepare(2 * i + 2, 0)
                    mix(i, 0)
                    prepare(2 * i + 3, 1)
                    mix(i, 1)
                mix(CHUNKS // 2 - 1, 0)
                mix(CHUNKS // 2 - 1, 1)

            def read_sums(b):
                half, q = b // PAIRS, b % PAIRS
                dve.wait_ge(contracted[STEPS - 1], (b + 1) * ITERS + START)
                dve.tensor_copy(hT[:, q, half * SPAN:(half + 1) * SPAN], psA[:, :]).then_inc(sums_copied, 1)
                dve.tensor_scalar(inv_den[:], den, 1e-30, None, ALU.max).then_inc(evacuated, 1)
                dve.wait_ge(evacuated, b + 1)

            def invert(r):
                at = slice(r * BANK, (r + 1) * BANK)
                dve.reciprocal(inv_den[:, at], inv_den[:, at]).then_inc(inv_ready, 1)

            def scale_sums(b):
                half, q = b // PAIRS, b % PAIRS
                here = hT[:, q, half * SPAN:(half + 1) * SPAN]
                if b:
                    dve.wait_ge(inv_stored, 16 * b)
                for r in range(2):
                    dve.wait_ge(spread_done, 2 * b + r + 1)
                    dve.tensor_copy(inv_blk[:, 2 * r * BANK:2 * (r + 1) * BANK], spread_ps).then_inc(inv_copied, 1)
                dve.wait_ge(inv_copied, 2 * b + 2)
                dve.wait_ge(sums_copied, b + 1)
                dve.tensor_tensor(here, here, inv_blk[:], ALU.mult).then_inc(scaled, 1)
                dve.wait_ge(scaled, b + 1)
                for k in range(QUARTERS):
                    ins = dve.bn_stats(stats[:, q, half * QUARTERS + k], hT[:, q, half * SPAN + k * BANK:
                                                                           half * SPAN + (k + 1) * BANK])
                ins.then_inc(stats_done, 1)

            dve.wait_ge(dve_small, small[0])

            def take_bytes(b, j, t):
                n, use = b // PAIRS * ITERS + j, b * ITERS + j
                dve.wait_ge(adj_in[t], 16 * (n + 1))
                if t < 2:
                    dve.wait_ge(adj8_out[t + 2], 16 * n + START)
                    if b or not isinstance(j, int) or j:
                        dve.wait_ge(masked[t + 2], 2 * use)
                else:
                    dve.wait_ge(adj8_out[t - 2], 16 * (n + 1) + START)
                    dve.wait_ge(masked[t - 2], 2 * use + 2)
                dve.tensor_copy(mask8[:, t % 2], mask[:, t % 2]).then_inc(adj8_ready[t], 1)

            def first(b, j, t, last=False):
                half, q = b // PAIRS, b % PAIRS
                use = b * ITERS + j
                keep_lhs(use, t, j, q)
                if q == 0:
                    if t < STEPS - 1:
                        take_bytes(b, j, t + 1)
                    elif not last:
                        take_bytes(b, j + 1, 0)
                    dve.wait_ge(adj8_ready[t], half * ITERS + j + 1)
                else:
                    dve.wait_ge(mask_in[t], 16 * (half * ITERS + j + 1))
                mask_scores(0, use, t, mask8[:, t % 2])

            for b in range(BLOCKS):
                if b % PAIRS == 0:
                    take_bytes(b, 0, 0)
                for t in range(STEPS):
                    first(b, 0, t)
                    if b:
                        if t == 0:
                            read_sums(b - 1)
                        elif t < 3:
                            invert(t - 1)
                        else:
                            scale_sums(b - 1)
                with dve.Fori(1, ITERS - 1) as j:
                    for t in range(STEPS):
                        first(b, j, t)
                for t in range(STEPS):
                    first(b, ITERS - 1, t, last=True)
            read_sums(BLOCKS - 1)
            invert(0)
            invert(1)
            scale_sums(BLOCKS - 1)
            dve.wait_ge(stats_done, BLOCKS)
            dve.wait_ge(weights_in, SETUP_LOADS + 3 * 16)

            bn_coefficients(PARAMS.index("enc_g"), PARAMS.index("enc_b"))
            mlp("enc")
            dve.wait_ge(stats_done, BLOCKS + CHUNKS)
            bn_coefficients(PARAMS.index("enc_mlp_g"), PARAMS.index("enc_mlp_beta"))
            with dve.Fori(0, CHUNKS // 2) as i:
                for c in range(2):
                    dve.wait_ge(chunk["emb"]["mm"][c], i + START)
                    apply_bn(cin[:, c], 2 * i + c, chunk["emb"]["cin"][c])
            for c in range(2):
                dve.wait_ge(chunk["emb"]["act"][c], CHUNKS // 2 + START)

            def second(b, j, t):
                use = APP + b * ITERS + j
                keep_lhs(use, t, j, b % PAIRS)
                if t % 2 == 0:
                    dve.wait_ge(mask_in[t], 16 * (HALVES * ITERS + b * ITERS + j + 1))
                    mask_scores(1, use, t, mask8[:, t // 2])

            def scale_second(b):
                half, q = b // PAIRS, b % PAIRS
                dve.wait_ge(inv_in, 16 * (b + 1))
                dve.wait_ge(contracted[STEPS - 1], APP + (b + 1) * ITERS + START)
                dve.tensor_tensor(hT[:, q, half * SPAN:(half + 1) * SPAN], (psA, psB)[b % 2][:, :], inv_blk[:], ALU.mult
                                  ).then_inc(evacuated, 1)
                dve.wait_ge(evacuated, BLOCKS + b + 1)

            def elu(b):
                half, q = b // PAIRS, b % PAIRS
                here = hT[:, q, half * SPAN:(half + 1) * SPAN]
                dve.wait_ge(elu_exp, b + 1)
                dve.tensor_scalar(inv_blk[:], inv_blk[:], 1.0, -1.0, ALU.min, ALU.add).then_inc(elu_min, 1)
                dve.wait_ge(elu_min, b + 1)
                dve.scalar_tensor_tensor(out=here, in0=here, scalar=0.0, in1=inv_blk[:], op0=ALU.max, op1=ALU.add
                                         ).then_inc(elu_done, 1)

            for b in range(BLOCKS):
                for t in range(STEPS):
                    second(b, 0, t)
                    if b and t == 0:
                        scale_second(b - 1)
                if b:
                    elu(b - 1)
                with dve.Fori(1, ITERS) as j:
                    for t in range(STEPS):
                        second(b, j, t)
            scale_second(BLOCKS - 1)
            elu(BLOCKS - 1)
            dve.wait_ge(elu_done, BLOCKS)
            mlp("dec")
            dve.wait_ge(stats_done, BLOCKS + 2 * CHUNKS)
            bn_coefficients(PARAMS.index("dec_mlp_g"), PARAMS.index("dec_mlp_beta"))

            def layernorm(n, src, dst, done):
                for t in range(CT):
                    ins = dve.bn_stats(ln_stats[:, t], src[:, t])
                ins.then_inc(ln_small_done, 1)
                dve.wait_ge(ln_small_done, 3 * n + 1)
                dve.memset(ln_gate[:], 0.0)
                for t in range(CT):
                    ins = dve.bn_aggr(ln_mom[:, t], ln_stats[:, t])
                ins.then_inc(ln_small_done, 1)
                dve.wait_ge(ln_small_done, 3 * n + 2)
                dve.tensor_scalar(ln_small[:, 0], ln_mom[:, :, 1], LN_EPS, None, ALU.add).then_inc(ln_var, 1)
                dve.wait_ge(ln_rstd, n + 1)
                dve.scalar_tensor_tensor(out=ln_small[:, 2], in0=ln_mom[:, :, 0], scalar=-1.0, in1=ln_small[:, 1],
                                         op0=ALU.mult, op1=ALU.mult).then_inc(ln_small_done, 1)
                dve.wait_ge(ln_small_done, 3 * n + 3)
                for t in range(CT):
                    ins = dve.tensor_scalar(dst[:, t], src[:, t], ln_small[:, 1, t:t + 1], ln_small[:, 2, t:t + 1],
                                            ALU.mult, ALU.add)
                ins.then_inc(done, 1)

            def norm_and_sum(i, c):
                ch = 2 * i + c
                dve.wait_ge(turned[c], i + START)
                apply_bn(normed[:, c], ch, normed_ready[c])
                dve.wait_ge(turned[c], i + 1 + START)
                dve.wait_ge(x_in[c], 16 * (i + 1))
                dve.wait_ge(x2_turned[c], i + START)
                dve.wait_ge(x2_kept[c], i + START)
                dve.tensor_tensor(y[:, c], psA[:, 0:2 * BANK].rearrange("p (t f) -> p t f", t=CT), xin[:, c], ALU.add
                                  ).then_inc(summed[c], 1)
                dve.wait_ge(summed[c], i + 1 + START)
                layernorm(ch, y[:, c], y[:, c], x2_ready[c])

            def split(ch):
                dve.wait_ge(prod_copied, (ch + 1) * CT + START)
                src = product3[:]
                hi = q0[:, ds(ch * CT, CT), 0]
                lo = q0[:, ds(ch * CT, CT), 1]
                dve.tensor_copy(hi, src).then_inc(q_hi, 1)
                dve.wait_ge(q_hi, ch + 1)
                dve.tensor_tensor(lo, src, hi.bitcast(F32), ALU.subtract).then_inc(q_lo, 1)

            norm_and_sum(0, 0)
            with dve.Fori(0, CHUNKS // 2 - 1) as i:
                norm_and_sum(i, 1)
                split(2 * i)
                norm_and_sum(i + 1, 0)
                split(2 * i + 1)
            norm_and_sum(CHUNKS // 2 - 1, 1)
            split(CHUNKS - 2)
            split(CHUNKS - 1)

            for n in range(HOPS):
                last = n == HOPS - 1
                dst = (q1, q0)[n % 2]
                with dve.Fori(0, BLOCKS) as ib:
                    for c in range(2):
                        b = n * 2 * BLOCKS + 2 * ib + c
                        acc = (psA, psB)[c][:, :].rearrange("p (m k f) -> p m k f", m=CT, k=2)
                        dve.wait_ge(xw_in[c], 16 * (n * BLOCKS + ib + 1))
                        dve.wait_ge(hop_contracted[1], n * APP + ib * ITERS + (c + 1) * (ITERS // 2) + START)
                        if last:
                            dve.wait_ge(out_free, 2 * ib + c + START)
                        dve.tensor_tensor(xw[:, c], acc[:, :, 1], xw[:, c], ALU.add).then_inc(sum1, 1)
                        dve.wait_ge(sum1, b + 1)
                        dve.tensor_tensor(total[:], acc[:, :, 0], xw[:, c], ALU.add).then_inc(hop_evac[c], 1)
                        dve.wait_ge(hop_evac[c], n * BLOCKS + ib + 1 + START)
                        here = ds((2 * ib + c) * CT, CT)
                        if not last:
                            dve.tensor_copy(dst[:, here, 0], total[:]).then_inc(hop_hi, 1)
                            dve.wait_ge(hop_hi, b + 1)
                            dve.tensor_tensor(dst[:, here, 1], total[:], dst[:, here, 0].bitcast(F32), ALU.subtract
                                              ).then_inc(hop_q, 1)
                        else:
                            dve.tensor_tensor(total[:], total[:], x2[:, here], ALU.add).then_inc(sum2, 1)
                            dve.wait_ge(sum2, 2 * ib + c + 1)
                            layernorm(CHUNKS + 2 * ib + c, total, total, out_ready)

        @block.gpsimd
        def _(pool):
            for s in reused:
                pool.sem_inc(s, START)
            pool.sem_inc(started, 1)
            pool.memset(ident[:], 0.0).then_inc(ident0, 1)
            pool.wait_ge(ident0, 1)
            pool.affine_select(out=ident[:], in_=ident[:], compare_op=ALU.not_equal, fill=1.0, base=0,
                               pattern=[[-1, P]], channel_multiplier=1).then_inc(ident_set, 1)
            pool.wait_ge(consts_set, 1)

            def bn_pow(n):
                pool.wait_ge(var_ready, n + 1)
                pool.tensor_tensor(norm[:, 1], norm[:, 0], minus_half[:, 0:PAIRS], ALU.pow).then_inc(rstd_ready, 1)

            bn_pow(0)
            bn_pow(1)
            bn_pow(2)

            def ln_pow(n):
                pool.wait_ge(ln_var, n + 1)
                pool.tensor_tensor(ln_small[:, 1], ln_small[:, 0], minus_half[:], ALU.pow).then_inc(ln_rstd, 1)

            ln_pow(0)

            def store_products(i, c):
                ch = 2 * i + c
                pool.wait_ge(prod_copied, (ch + 1) * CT + START)
                pool.dma_start(xw_dram[ds(ch * CT, CT)].rearrange("t p k f -> p t (k f)"), products[c][:]
                               ).then_inc(prod_stored, 16)

            def free_products(i, c):
                pool.wait_ge(prod_stored, 16 * (2 * i + c + 1))
                pool.sem_inc(prod_free[c], 1)

            ln_pow(1)
            store_products(0, 0)
            with pool.Fori(0, CHUNKS // 2 - 1) as i:
                ln_pow(2 * i + 2)
                free_products(i, 0)
                store_products(i, 1)
                ln_pow(2 * i + 3)
                free_products(i, 1)
                store_products(i + 1, 0)
            free_products(CHUNKS // 2 - 1, 0)
            store_products(CHUNKS // 2 - 1, 1)
            free_products(CHUNKS // 2 - 1, 1)
            with pool.Fori(0, CHUNKS) as b:
                ln_pow(CHUNKS + b)
                pool.wait_ge(out_ready, b + 1)
                pool.dma_start(out_view[ds(b, 1)].rearrange("a p t f -> p (a t) f"), total[:]).then_inc(out_stored, 16)
                pool.wait_ge(out_stored, 16 * (b + 1))
                pool.sem_inc(out_free, 1)


def kernel(**inputs):
    import numpy as np
    import concourse.bacc as bacc
    from concourse.bass_utils import run_bass_kernel_spmd

    g = {k.replace("L0_gnn_", ""): np.asarray(v) for k, v in inputs.items()}
    pairs = lambda a: np.ascontiguousarray(a.reshape(PAIRS, 2 * D, -1).transpose(1, 0, 2))
    vec = [g[k] for k in ("enc_bn_gamma", "enc_bn_beta", "enc_mlp_b", "enc_mlp_bn_gamma", "enc_mlp_bn_beta",
                          "dec_mlp_b", "dec_mlp_bn_gamma", "dec_mlp_bn_beta")]
    W, V = g["W"], g["V"]
    arrays = {
        "x": np.ascontiguousarray(g["x"]),
        "xT": np.ascontiguousarray(g["x"].T),
        "adjT": np.ascontiguousarray(
            g["adj"].reshape(HALVES, SPAN, NT, P).transpose(0, 2, 3, 1).reshape(HALVES * NT, P, SPAN)),
        "head_w": pairs(W),
        "head_wT": pairs(np.ascontiguousarray(W.transpose(0, 2, 1))),
        "v1": np.ascontiguousarray(V[:, 0, :, 0].reshape(PAIRS, P).T),
        "v2_row": np.ascontiguousarray(V[:, 1, :, 0].reshape(F)),
        "params": np.ascontiguousarray(np.stack(vec).reshape(len(vec), PAIRS, P).transpose(2, 0, 1)),
        "enc_wT": np.ascontiguousarray(g["enc_mlp_W"].T.reshape(PAIRS, P, F).transpose(1, 0, 2)),
        "dec_wT": np.ascontiguousarray(g["dec_mlp_W"].T.reshape(PAIRS, P, F).transpose(1, 0, 2)),
        "hop_w": np.ascontiguousarray(g["L1_gnn_weight"].reshape(4, PAIRS, P, F).transpose(2, 1, 0, 3)),
    }
    nc = bacc.Bacc("TRN2", target_bir_lowering=False, num_devices=1)
    aps = [nc.dram_tensor(f"in_{k}", a.shape, mybir.dt.from_np(a.dtype), kind="ExternalInput").ap()
           for k, a in arrays.items()]
    out = nc.dram_tensor("out_dram", [N, F], F32, kind="ExternalOutput").ap()
    gnn_kernel(nc, *aps, out)
    r = run_bass_kernel_spmd(nc, [{f"in_{k}": a for k, a in arrays.items()}], core_ids=[0])
    return r.results[0]["out_dram"]
```

```python
from contextlib import ExitStack

import concourse.bass as bass
from concourse import mybir
from concourse.alu_op_type import AluOpType as ALU

ACT = mybir.ActivationFunctionType
F32 = mybir.dt.float32
F32R = mybir.dt.float32r
U8 = mybir.dt.uint8
ds = bass.ds

P = 128
N = 4096
F = 256
H = 4
D = F // H
PAIRS = F // P
NT = N // P
SPAN = 2048
HALVES = N // SPAN
BLOCKS = HALVES * PAIRS
BANK = 512
STEPS = 4
ITERS = NT // STEPS
APP = BLOCKS * ITERS
CHUNK = 512
CHUNKS = N // CHUNK
CT = CHUNK // P
HOPS = 3
START = 1
SETUP_LOADS = 16 * 6
QUARTERS = SPAN // BANK
BN_EPS = 1e-6
LN_EPS = 1e-5
PARAMS = ["enc_g", "enc_b", "enc_mlp_b", "enc_mlp_g", "enc_mlp_beta", "dec_mlp_b", "dec_mlp_g", "dec_mlp_beta"]


def gnn_kernel(nc, x, xT, adjT, head_w, head_wT, v1, v2_row, params, enc_wT, dec_wT, hop_w, out):
    f1_dram = nc.dram_tensor("f1_scratch", [H, N], F32, kind="Internal").ap()
    adj8_dram = nc.dram_tensor("adj8_scratch", [((CHUNKS + 1) * ITERS * P * STEPS), BANK], U8, kind="Internal").ap()
    scores_dram = nc.dram_tensor("scores_scratch", [APP, 2, P, 2 * SPAN], F32, kind="Internal").ap()
    inv_dram = nc.dram_tensor("inv_scratch", [BLOCKS, P, SPAN], F32, kind="Internal").ap()
    xw_dram = nc.dram_tensor("xw_scratch", [NT, P, HOPS, F], F32, kind="Internal").ap()

    base = nc.sbuf_base + (-nc.sbuf_base) % 64
    end = nc.sbuf_usable_end

    def placer(at):
        def place(name, shape, dt=F32, size=4):
            n = size
            for s in shape[1:]:
                n *= s
            assert place.at + n <= end, (name, place.at + n - end)
            t = nc.alloc_sbuf_tensor_at(name, shape, dt, offset=place.at)
            place.at += n + (-n) % 32
            return t
        place.at = at
        return place

    const = placer(base)
    w_sb = const("w_sb", [P, PAIRS, P])
    wT_sb = const("wT_sb", [P, PAIRS, P])
    v_sb = const("v_sb", [P, PAIRS])
    wv = const("wv", [P, PAIRS])
    wv_cols = const("wv_cols", [P, PAIRS, P])
    par = const("par", [P, len(PARAMS), PAIRS])
    encw = const("encw", [P, PAIRS, F])
    decw = const("decw", [P, PAIRS, F])
    ident = const("ident", [P, P])
    ones = const("ones", [P, 32])
    minus_half = const("minus_half", [P, CT])
    spread = const("spread", [P, 2, P])
    f2_half = const("f2_half", [P, NT, H])
    stats = const("stats", [P, PAIRS, CHUNKS, 6])
    moments = const("moments", [P, PAIRS, 2])
    norm = const("norm", [P, 4, PAIRS])
    ln_stats = const("ln_stats", [P, CT, 6])
    ln_mom = const("ln_mom", [P, CT, 2])
    ln_small = const("ln_small", [P, 3, CT])
    ln_gate = const("ln_gate", [P, 1])
    region = const.at

    att = placer(region)
    hT = att("hT", [P, PAIRS, N])
    values = att("values", [P, NT, F])
    f1_rows = att("f1_rows", [P, PAIRS, 2, SPAN])
    ring = att("ring", [P, STEPS, 2, SPAN])
    inv_at = att.at
    inv_den = att("inv_den", [P, 2 * BANK])
    inv_blk = att("inv_blk", [P, SPAN])
    mask_at = att.at
    mask = att("mask", [P, 2, SPAN])
    mask8 = att("mask8", [P, 2, SPAN], U8, 1)
    lhs = att("lhs", [P, STEPS, P])
    v2_b = att("v2_b", [P, F])

    mid = placer(region + 4 * (PAIRS * N + NT * F + 2 * SPAN))
    cin = mid("cin", [P, 2, PAIRS, CHUNK])
    mid = placer(mask_at)
    cexp = mid("cexp", [P, 2, PAIRS, CHUNK])
    crelu = mid("crelu", [P, 2, PAIRS, CHUNK])
    early = placer(inv_at)
    f1_stage = early("f1_stage", [P, 2, CHUNK])
    prod = early("prod", [P, 2, CT, F])

    hop = placer(region)
    q1 = hop("q1", [P, NT, 2, F], F32R)
    q0 = hop("q0", [P, NT, 2, F], F32R)
    x2 = hop("x2", [P, NT, F])
    tail = hop.at
    adj8 = hop("adj8", [P, 2, STEPS * BANK], U8, 1)
    adjr = hop("adjr", [P, 2, STEPS, BANK], F32R)
    xw = hop("xw", [P, 2, CT, F])
    total = hop("total", [P, CT, F])

    ln = placer(region + 4 * PAIRS * N)
    hopw = ln("hopw", [P, PAIRS, 4 * F])
    xin = ln("xin", [P, 2, CT, F])
    product3 = ln("product3", [P, CT, F])
    lt = placer(tail)
    normed = lt("normed", [P, 2, PAIRS, CHUNK])
    y = lt("y", [P, 2, CT, F])
    x2T = lt("x2T", [P, 2, PAIRS, CHUNK])
    products = [ln("products0", [P, CT, HOPS * F]), lt("products1", [P, CT, HOPS * F])]

    ctx = ExitStack()
    with ctx:
        psA = ctx.enter_context(nc.psum_tensor("psA", [P, 4 * BANK], F32))
        psB = ctx.enter_context(nc.psum_tensor("psB", [P, 4 * BANK], F32))

        def sem(name):
            return ctx.enter_context(nc.semaphore(name))

        def slots(name, n=2):
            return [sem(f"{name}{i}") for i in range(n)]

        weights_zeroed = sem("weights_zeroed")
        started = sem("started")
        weights_in = sem("weights_in")
        consts_set = sem("consts_set")
        ident0 = sem("ident0")
        ident_set = sem("ident_set")
        wv_mm = sem("wv_mm")
        wv_ready = sem("wv_ready")
        set_in = slots("set_in")
        set_mm = slots("set_mm")
        f1_mm = slots("f1_mm")
        set_copied = slots("set_copied")
        f1_staged = slots("f1_staged")
        f1_stored = slots("f1_stored")
        f2_prod = slots("f2_prod")
        f2_sum = slots("f2_sum")
        f2_ready = sem("f2_ready")
        f1_in = slots("f1_in")
        adj_in = slots("adj_in", STEPS)
        adj8_ready = slots("adj8_ready", STEPS)
        adj8_out = slots("adj8_out", STEPS)
        tanh_done = slots("tanh_done", STEPS)
        exp_done = slots("exp_done", STEPS)
        masked = slots("masked", STEPS)
        lhs_ready = slots("lhs_ready", STEPS)
        contracted = slots("contracted", STEPS)
        spilled = slots("spilled", STEPS)
        scores_in = slots("scores_in", STEPS)
        mask_in = slots("mask_in", STEPS)
        sums_copied = sem("sums_copied")
        evacuated = sem("evacuated")
        inv_ready = sem("inv_ready")
        spread_done = sem("spread_done")
        inv_copied = sem("inv_copied")
        inv_stored = sem("inv_stored")
        inv_in = sem("inv_in")
        scaled = sem("scaled")
        elu_exp = sem("elu_exp")
        elu_min = sem("elu_min")
        elu_done = sem("elu_done")
        chunk = {}
        for tag, names in (("enc", ("cin", "mm", "act", "mixed", "h")), ("emb", ("cin", "mm", "act")),
                           ("dec", ("mm", "act", "mixed", "h"))):
            chunk[tag] = {n: slots(f"{tag}_{n}") for n in names}
        stats_done = sem("stats_done")
        var_ready = sem("var_ready")
        rstd_ready = sem("rstd_ready")
        coefficients_ready = sem("coefficients_ready")
        dve_small = sem("dve_small")
        hopw_in = sem("hopw_in")
        x_in = slots("x_in")
        normed_ready = slots("normed_ready")
        turned = slots("turned")
        summed = slots("summed")
        ln_var = sem("ln_var")
        ln_rstd = sem("ln_rstd")
        ln_small_done = sem("ln_small_done")
        x2_ready = slots("x2_ready")
        x2_turned = slots("x2_turned")
        x2T_ready = slots("x2T_ready")
        x2_kept = slots("x2_kept")
        prod_mm = sem("prod_mm")
        prod_copied = sem("prod_copied")
        prod_stored = sem("prod_stored")
        prod_free = slots("prod_free")
        q_hi = sem("q_hi")
        q_lo = sem("q_lo")
        hop_adj_in = slots("hop_adj_in")
        cast_done = slots("cast_done")
        hop_contracted = slots("hop_contracted")
        xw_in = slots("xw_in")
        hop_evac = slots("hop_evac")
        sum1 = sem("sum1")
        sum2 = sem("sum2")
        hop_hi = sem("hop_hi")
        hop_q = sem("hop_q")
        out_ready = sem("out_ready")
        out_stored = sem("out_stored")
        out_free = sem("out_free")

        reused = [set_mm, set_copied, f1_staged, f1_stored, f2_sum, contracted, adj8_out, spilled, summed,
                  turned, x2_turned, x2_kept, x2T_ready, hop_evac, cast_done, hop_contracted]
        reused = [s for group in reused for s in group]
        reused += [*prod_free, q_lo, prod_copied, out_free]
        reused += [s for tag in chunk for n in ("act", "mm", "h") if n in chunk[tag] for s in chunk[tag][n]]

        block = ctx.enter_context(nc.Block())

        xT_view = xT.rearrange("(q p) n -> p q n", p=P)
        x_view = x.rearrange("(c t p) f -> c p t f", t=CT, p=P)
        out_view = out.rearrange("(c t p) f -> c p t f", t=CT, p=P)

        den = psB[:, 0:2 * BANK]
        spread_ps = psB[:, 2 * BANK:4 * BANK]
        chunk_ps = [psA[:, s * 2 * BANK:(s + 1) * 2 * BANK] for s in range(2)]

        @block.sync
        def _(sp):
            def load_adj(half, j, t, slot):
                sp.dma_start(mask[:, slot], adjT[ds(half * NT + j * STEPS + t, 1)].rearrange("a p x -> p (a x)")
                             ).then_inc(adj_in[t % STEPS], 16)

            sp.dma_start(v_sb[:], v1).then_inc(weights_in, 16)
            sp.wait_ge(weights_zeroed, 2)
            for dst, src in ((wT_sb, head_wT), (w_sb, head_w)):
                for hh in range(2):
                    a = slice(D * hh, D * (hh + 1))
                    sp.dma_start(dst[a, :, a], src[a]).then_inc(weights_in, 16)
            sp.dma_start(v2_b[:], v2_row.partition_broadcast(P)).then_inc(weights_in, 16)
            sp.wait_ge(started, 1)
            with sp.Fori(0, CHUNKS // 2) as i:
                for c in range(2):
                    sp.wait_ge(set_mm[c], i + START)
                    sp.dma_start(cin[:, c], xT_view[:, :, ds((2 * i + c) * CHUNK, CHUNK)]).then_inc(set_in[c], 16)
            with sp.Fori(CHUNKS // 4, CHUNKS // 2) as i:
                for c in range(2):
                    sp.wait_ge(f1_staged[c], i + 1 + START)
                    sp.dma_start(f1_dram[:, ds((2 * i + c) * CHUNK, CHUNK)], f1_stage[0:P:P // H, c]
                                 ).then_inc(f1_stored[c], 16)

            def adj8_step(half, j, t):
                span = QUARTERS * ITERS * P * STEPS
                return adj8_dram[ds(half * span + j * (P * STEPS) + t + 1, span)].rearrange(
                    "(h p y) x -> p h y x", h=QUARTERS, y=STEPS)[0:P, :, 0]

            def load_mask(at, t, slot):
                sp.dma_start(mask8[:, slot].rearrange("p (h x) -> p h x", h=QUARTERS), at).then_inc(mask_in[t], 16)

            def spill(it, t):
                sp.dma_start(scores_dram[ds(it, 1), t // 2].rearrange("a p x -> p (a x)"),
                             ring[:, t].rearrange("p h i -> p (h i)")).then_inc(spilled[t], 16)

            def read_adjacency(b, j, last):
                half, it = b // PAIRS, b * ITERS + j
                for t in range(STEPS):
                    sp.wait_ge(adj8_ready[t], half * ITERS + j + 1)
                    if t < 2:
                        load_adj(half, j, t + 2, t)
                    elif not last:
                        sp.dma_start(mask[:, t - 2], adjT[ds(half * NT + j * STEPS + t + 2, 1)].rearrange(
                            "a p x -> p (a x)")).then_inc(adj_in[t - 2], 16)
                    sp.dma_start(adj8_step(half, j, t), mask8[:, t % 2].rearrange("p (h x) -> p h x", h=QUARTERS)
                                 ).then_inc(adj8_out[t], 16)
                    if t % 2 == 0 and (t or not isinstance(j, int) or j):
                        before = (it, t - 1) if t else (it - 1, STEPS - 1)
                        sp.wait_ge(masked[before[1]], 2 * before[0] + 2)
                        spill(*before)
                    if last and t > 1:
                        sp.wait_ge(adj8_out[t - 2], 16 * (half + 1) * ITERS + START)
                        sp.wait_ge(adj8_out[t], 16 * (half + 1) * ITERS + START)
                        sp.wait_ge(masked[t], 2 * it + 2)
                        load_mask(adj8_step(half, 0, t - 2), t - 2, t - 2)
                if last:
                    spill(it, STEPS - 1)

            def read_masks(b, j, last):
                half, it = b // PAIRS, b * ITERS + j
                for t in range(STEPS):
                    ahead = t + 2 - STEPS * (t >= 2)
                    load = t < 2 or not last
                    at = adj8_step(half, j + (t >= 2), ahead) if load else None
                    sp.wait_ge(masked[t], 2 * it + 2)
                    if load:
                        load_mask(at, ahead, t % 2)
                    if t % 2:
                        spill(it, t)

            def store_inv(b):
                sp.wait_ge(inv_copied, 2 * b + 2)
                sp.dma_start(inv_dram[b], inv_blk[:]).then_inc(inv_stored, 16)

            for t in range(2):
                load_adj(0, 0, t, t)
            sp.dma_start(par[:], params).then_inc(weights_in, 16)
            sp.dma_start(encw[:], enc_wT).then_inc(weights_in, 16)
            sp.dma_start(decw[:], dec_wT).then_inc(weights_in, 16)
            for b in range(BLOCKS):
                half = b // PAIRS
                body = read_masks if b % PAIRS else read_adjacency
                if b % PAIRS and b + 1 < BLOCKS:
                    for t in range(2):
                        load_adj(half + 1, 0, t, t)
                body(b, 0, False)
                with sp.Fori(1, ITERS - 1) as j:
                    body(b, j, False)
                if b:
                    store_inv(b - 1)
                body(b, ITERS - 1, True)
            store_inv(BLOCKS - 1)

            def second(b, j):
                half, it = b // PAIRS, b * ITERS + j
                for t in range(STEPS):
                    if t % 2:
                        sp.wait_ge(contracted[t], APP + it + START)
                        sp.dma_start(ring[:, t].rearrange("p h i -> p (h i)"),
                                     scores_dram[ds(it, 1), t // 2].rearrange("a p x -> p (a x)")
                                     ).then_inc(scores_in[t], 16)
                    else:
                        at = adj8_step(half, j, t)
                        sp.wait_ge(masked[t], 2 * (APP + it))
                        load_mask(at, t, t // 2)

            for t in (1, 3):
                sp.wait_ge(spilled[t], 16 * APP + START)
                sp.wait_ge(masked[t], 2 * APP)
            for b in range(BLOCKS):
                with sp.Fori(0, ITERS - 1) as j:
                    second(b, j)
                sp.wait_ge(inv_stored, 16 * BLOCKS)
                if b:
                    sp.wait_ge(elu_done, b)
                sp.dma_start(inv_blk[:], inv_dram[b]).then_inc(inv_in, 16)
                second(b, ITERS - 1)

            sp.wait_ge(contracted[STEPS - 1], 2 * APP + START)
            sp.dma_start(hopw[:].rearrange("p q (k f) -> p q k f", k=4), hop_w).then_inc(hopw_in, 16)
            with sp.Fori(0, CHUNKS // 2) as i:
                for c in range(2):
                    sp.wait_ge(summed[c], i + START)
                    sp.dma_start(xin[:, c], x_view[ds(2 * i + c, 1)].rearrange("a p t f -> p (a t) f")
                                 ).then_inc(x_in[c], 16)

            sp.wait_ge(turned[1], CHUNKS // 2 + START)
            for n in range(HOPS):
                with sp.Fori(0, BLOCKS) as ib:
                    for c in range(2):
                        with sp.Fori(0, ITERS // 2) as jp:
                            for s in range(2):
                                sp.wait_ge(cast_done[s], n * APP + ib * ITERS + c * (ITERS // 2) + jp + START)
                                sp.dma_start(adj8[:, s], adj8_dram[
                                    ds(((2 * ib + c) * ITERS + 2 * jp + s) * (P * STEPS) + 1, P * STEPS)].rearrange(
                                        "(p t) x -> p (t x)", p=P)).then_inc(hop_adj_in[s], 16)
                        if n == 0:
                            for k in range(2):
                                sp.wait_ge(prod_free[k], CHUNKS // 2 + START)
                        sp.wait_ge(hop_evac[c], n * BLOCKS + ib + START)
                        sp.dma_start(xw[:, c], xw_dram[ds((2 * ib + c) * CT, CT), :, HOPS - 1 - n].rearrange(
                            "t p f -> p t f")).then_inc(xw_in[c], 16)

        @block.tensor
        def _(pe):
            def head_products(i, c, w, copied, done):
                pe.wait_ge(copied[c], i + START)
                for t in range(CT):
                    for q in range(PAIRS):
                        at = t * F + q * P
                        mm = pe.matmul(chunk_ps[c][:, at:at + P], cin[:, c, q, t * P:(t + 1) * P], w[:, q, :],
                                       start=True, stop=True)
                mm.then_inc(done[c], 1)

            pe.wait_ge(started, 1)
            pe.wait_ge(weights_in, SETUP_LOADS)
            for q in range(PAIRS):
                mm = pe.matmul(psB[:, q:q + 1], wT_sb[:, q, :], v_sb[:, q:q + 1], start=True, stop=True)
            mm.then_inc(wv_mm, 1)
            pe.wait_ge(wv_ready, 1)
            with pe.Fori(0, CHUNKS // 2) as i:
                for c in range(2):
                    pe.wait_ge(set_in[c], 16 * (i + 1))
                    pe.wait_ge(f1_staged[c], i + START)
                    for q in range(PAIRS):
                        mm = pe.matmul(psB[:, c * BANK:(c + 1) * BANK], wv_cols[:, q, :], cin[:, c, q, :],
                                       start=q == 0, stop=q == PAIRS - 1)
                    mm.then_inc(f1_mm[c], 1)
                    head_products(i, c, w_sb, set_copied, set_mm)

            def step(use, t, a, acc, first, last):
                pe.wait_ge(lhs_ready[t], use + 1)
                if a == 1 and t % 2:
                    pe.wait_ge(scores_in[t], 16 * (use - APP + 1))
                else:
                    pe.wait_ge(masked[t], 2 * use + 2)
                for k in range(QUARTERS):
                    at = slice(k * BANK, (k + 1) * BANK)
                    for hh in range(2):
                        mm = pe.matmul(acc[D * hh:D * hh + D, at], lhs[:, t, hh * D:(hh + 1) * D], ring[:, t, hh, at],
                                       start=first, stop=last, tile_position=(0, D * hh))
                if a == 0:
                    for k in range(QUARTERS):
                        for hh in range(2):
                            g = 32 * (2 * hh + k % 2)
                            mm = pe.matmul(den[g:g + 32, k // 2 * BANK:(k // 2 + 1) * BANK], ones[:],
                                           ring[:, t, hh, k * BANK:(k + 1) * BANK],
                                           start=first, stop=last, tile_position=(0, g))
                mm.then_inc(contracted[t], 1)

            def spread_inv(b, r):
                pe.wait_ge(inv_ready, 2 * b + r + 1)
                if 2 * b + r:
                    pe.wait_ge(inv_copied, 2 * b + r)
                for k in range(2):
                    mm = pe.matmul(spread_ps[:, k * BANK:(k + 1) * BANK], spread[:, k, :],
                                   inv_den[:, r * BANK:(r + 1) * BANK], start=True, stop=True)
                mm.then_inc(spread_done, 1)

            def application(a):
                for b in range(BLOCKS):
                    acc = (psA, psB)[b % 2] if a else psA
                    if a == 0 and b:
                        pe.wait_ge(evacuated, b)
                    elif b >= 2:
                        pe.wait_ge(evacuated, BLOCKS + b - 1)
                    use = a * APP + b * ITERS
                    for t in range(STEPS):
                        step(use, t, a, acc, t == 0, False)
                        if a == 0 and b and t >= 2:
                            spread_inv(b - 1, t - 2)
                    with pe.Fori(1, ITERS - 1) as j:
                        for t in range(STEPS):
                            step(use + j, t, a, acc, False, False)
                    for t in range(STEPS):
                        step(use + ITERS - 1, t, a, acc, False, t == STEPS - 1)
                if a == 0:
                    for r in range(2):
                        spread_inv(BLOCKS - 1, r)

            def mlp(tag, w):
                s = chunk[tag]
                for half in range(HALVES):
                    if tag == "dec":
                        pe.wait_ge(elu_done, (half + 1) * PAIRS)
                    with pe.Fori(half * CHUNKS // 4, (half + 1) * CHUNKS // 4) as i:
                        for c in range(2):
                            if tag == "enc":
                                pe.wait_ge(s["cin"][c], i + 1)
                            pe.wait_ge(s["act"][c], i + START)
                            for o in range(PAIRS):
                                for q in range(PAIRS):
                                    mm = pe.matmul(chunk_ps[c][:, o * BANK:(o + 1) * BANK],
                                                   w[:, q, o * P:(o + 1) * P],
                                                   hT[:, q, ds((2 * i + c) * CHUNK, CHUNK)],
                                                   start=q == 0, stop=q == PAIRS - 1)
                            mm.then_inc(s["mm"][c], 1)

            application(0)
            pe.wait_ge(weights_in, SETUP_LOADS + 3 * 16)
            pe.wait_ge(scaled, BLOCKS + 1)
            mlp("enc", encw)
            with pe.Fori(0, CHUNKS // 2) as i:
                for c in range(2):
                    pe.wait_ge(chunk["emb"]["cin"][c], i + 1)
                    head_products(i, c, wT_sb, chunk["emb"]["act"], chunk["emb"]["mm"])
            application(1)
            pe.wait_ge(evacuated, 2 * BLOCKS - 1)
            mlp("dec", decw)

            def turn(i, c):
                pe.wait_ge(normed_ready[c], i + 1)
                if c:
                    pe.wait_ge(summed[0], i + 1 + START)
                else:
                    pe.wait_ge(summed[1], i + START)
                for t in range(CT):
                    for q in range(PAIRS):
                        at = t * F + q * P
                        mm = pe.transpose(psA[:, at:at + P], normed[:, c, q, t * P:(t + 1) * P], ident[:])
                mm.then_inc(turned[c], 1)

            def turn_x2(i, c):
                pe.wait_ge(x2_ready[c], i + 1)
                if c:
                    pe.wait_ge(x2T_ready[0], i + 1 + START)
                else:
                    pe.wait_ge(x2T_ready[1], i + START)
                for t in range(CT):
                    for q in range(PAIRS):
                        at = 2 * BANK + q * CHUNK + t * P
                        mm = pe.transpose(psA[:, at:at + P], y[:, c, t, q * P:(q + 1) * P], ident[:])
                mm.then_inc(x2_turned[c], 1)

            def hop_products(i, c, last):
                pe.wait_ge(x2T_ready[c], i + 1 + START)
                for t in range(CT):
                    before = 2 * i * CT + c * CT + t
                    pe.wait_ge(prod_copied, (before - 1 if c or t >= 2 else 2 * i * CT) + START)
                    for half in range(2):
                        for q in range(PAIRS):
                            mm = pe.matmul(psB[:, (2 * (t % 2) + half) * BANK:(2 * (t % 2) + half + 1) * BANK],
                                           x2T[:, c, q, t * P:(t + 1) * P], hopw[:, q, half * BANK:(half + 1) * BANK],
                                           start=q == 0, stop=q == PAIRS - 1)
                    mm.then_inc(prod_mm, 1)
                    if t == 0 and not last:
                        turn(i + 1, c)
                    if t == 1 and not (last and c):
                        turn_x2(i + c, 1 - c)

            pe.wait_ge(hopw_in, 16)
            pe.wait_ge(ident_set, 1)
            turn(0, 0)
            turn(0, 1)
            turn_x2(0, 0)
            with pe.Fori(0, CHUNKS // 2 - 1) as i:
                for c in range(2):
                    hop_products(i, c, False)
            for c in range(2):
                hop_products(CHUNKS // 2 - 1, c, True)

            def contract(n, ib, c, jp, s, first, last):
                src = (q0, q1)[n % 2]
                acc = (psA, psB)[c]
                use = n * APP + ib * ITERS + c * (ITERS // 2) + jp
                pe.wait_ge(cast_done[s], use + 1 + START)
                for t in range(STEPS):
                    j = (2 * jp + s) * STEPS + t
                    for m in range(CT):
                        mm = pe.matmul(acc[:, m * BANK:(m + 1) * BANK], adjr[:, s, t, m * P:(m + 1) * P],
                                       src[:, ds(j, 1)].rearrange("p a k f -> p (a k f)"),
                                       start=first and t == 0, stop=last and t == STEPS - 1)
                mm.then_inc(hop_contracted[s], 1)

            pe.wait_ge(q_lo, CHUNKS + START)
            pe.wait_ge(q_hi, CHUNKS)
            for n in range(HOPS):
                if n:
                    pe.wait_ge(hop_q, 2 * BLOCKS * n - 1)
                with pe.Fori(0, BLOCKS) as ib:
                    for c in range(2):
                        pe.wait_ge(hop_evac[c], n * BLOCKS + ib + START)
                        contract(n, ib, c, 0, 0, True, False)
                        contract(n, ib, c, 0, 1, False, False)
                        with pe.Fori(1, ITERS // 2 - 1) as jp:
                            contract(n, ib, c, jp, 0, False, False)
                            contract(n, ib, c, jp, 1, False, False)
                        contract(n, ib, c, ITERS // 2 - 1, 0, False, False)
                        if n:
                            pe.wait_ge(hop_q, 2 * BLOCKS * n)
                        contract(n, ib, c, ITERS // 2 - 1, 1, False, True)

        @block.scalar
        def _(act):
            def copy_values(i, c, mm, done):
                act.wait_ge(mm[c], i + 1 + START)
                act.activation(values[:, ds((2 * i + c) * CT, CT), :].rearrange("p t f -> p (t f)"), chunk_ps[c],
                               ACT.Copy).then_inc(done[c], 1)

            act.wait_ge(started, 1)
            with act.Fori(0, CHUNKS // 4) as i:
                for c in range(2):
                    act.wait_ge(f1_mm[c], i + 1)
                    act.wait_ge(f1_stored[c], 16 * i + START)
                    act.activation(f1_stage[:, c], psB[:, c * BANK:(c + 1) * BANK], ACT.Copy).then_inc(f1_staged[c], 1)
                    copy_values(i, c, set_mm, set_copied)
                    act.wait_ge(f1_staged[c], i + 1 + START)
                    act.dma_start(f1_dram[:, ds((2 * i + c) * CHUNK, CHUNK)],
                                  f1_stage[0:P:P // H, c]).then_inc(f1_stored[c], 16)

            def load_f1(b):
                half, q = b // PAIRS, b % PAIRS
                for hh in range(2):
                    act.dma_start(f1_rows[:, q, hh], f1_dram[2 * q + hh, half * SPAN:(half + 1) * SPAN]
                                  .partition_broadcast(P)).then_inc(f1_in[hh], 16)

            for c in range(2):
                act.wait_ge(f1_stored[c], 16 * CHUNKS // 4 + START)
            load_f1(0)

            def exps(use, t):
                both = ring[:, t].rearrange("p h i -> p (h i)")
                act.wait_ge(tanh_done[t], 2 * use + 2)
                act.activation(both, both, ACT.Exp, scale=0.5).then_inc(exp_done[t], 1)

            def scores(a, b, j, t):
                q, it = b % PAIRS, b * ITERS + j
                use = a * APP + it
                act.wait_ge(contracted[t], use + START)
                if t % 2:
                    act.wait_ge(spilled[t], 16 * it + START)
                for hh in range(2):
                    if isinstance(j, int):
                        act.wait_ge(f1_in[hh], 16 * (a * BLOCKS + b + 1))
                    act.activation(ring[:, t, hh], f1_rows[:, q, hh], ACT.Tanh,
                                   bias=f2_half[:, ds(j * STEPS + t, 1), 2 * q + hh], scale=0.5
                                   ).then_inc(tanh_done[t], 1)
                    if a == 0 and hh == 0 and (b or t or not isinstance(j, int) or j):
                        exps(use if t else use - 1, (t - 1) % STEPS)
                if a == 1:
                    for hh in range(2):
                        act.wait_ge(tanh_done[t], 2 * use + hh + 1)
                        act.activation(ring[:, t, hh], ring[:, t, hh], ACT.Exp, scale=0.5).then_inc(exp_done[t], 1)

            def mlp(tag, bias):
                s = chunk[tag]

                def prepare(ch, c):
                    if tag == "enc":
                        for q in range(PAIRS):
                            here = hT[:, q, ds(ch * CHUNK, CHUNK)]
                            ins = act.activation(here, here, ACT.Identity, bias=norm[:, 3, q:q + 1],
                                                 scale=norm[:, 2, q:q + 1])
                        ins.then_inc(s["cin"][c], 1)

                def chunk_elu(i, c):
                    act.wait_ge(s["mm"][c], i + 1 + START)
                    act.wait_ge(s["h"][c], i + START)
                    for o in range(PAIRS):
                        src = chunk_ps[c][:, o * BANK:(o + 1) * BANK]
                        act.activation(cexp[:, c, o], src, ACT.Exp, bias=par[:, bias, o:o + 1])
                        ins = act.activation(crelu[:, c, o], src, ACT.Relu, bias=par[:, bias, o:o + 1])
                    ins.then_inc(s["act"][c], 1)

                prepare(0, 0)
                prepare(1, 1)
                with act.Fori(0, CHUNKS // 2 - 1) as i:
                    for c in range(2):
                        prepare(2 * i + 2 + c, c)
                        chunk_elu(i, c)
                for c in range(2):
                    chunk_elu(CHUNKS // 2 - 1, c)

            act.wait_ge(f2_ready, 1)
            for b in range(BLOCKS):
                for t in range(STEPS):
                    scores(0, b, 0, t)
                    if t == 1:
                        if b == 0:
                            for c in range(2):
                                act.wait_ge(set_mm[c], CHUNKS // 2 + START)
                                act.wait_ge(f1_stored[c], 16 * CHUNKS // 2 + START)
                        load_f1((b + 1) % BLOCKS)
                with act.Fori(1, ITERS) as j:
                    if b == 0:
                        act.wait_ge(f2_ready, j + 1)
                    for t in range(STEPS):
                        scores(0, b, j, t)

            exps(APP - 1, STEPS - 1)

            for t in (0, 2):
                scores(1, 0, 0, t)
            act.wait_ge(weights_in, SETUP_LOADS + 3 * 16)
            act.wait_ge(coefficients_ready, 1)
            mlp("enc", PARAMS.index("enc_mlp_b"))
            with act.Fori(0, CHUNKS // 2) as i:
                for c in range(2):
                    copy_values(i, c, chunk["emb"]["mm"], chunk["emb"]["act"])

            def elu_exps(b):
                half, q = b // PAIRS, b % PAIRS
                act.wait_ge(evacuated, BLOCKS + b + 1)
                act.activation(inv_blk[:], hT[:, q, half * SPAN:(half + 1) * SPAN], ACT.Exp).then_inc(elu_exp, 1)

            for b in range(BLOCKS):
                if b:
                    for t in (0, 2):
                        scores(1, b, 0, t)
                    elu_exps(b - 1)
                if b + 1 < BLOCKS:
                    load_f1(b + 1)
                with act.Fori(1, ITERS) as j:
                    for t in (0, 2):
                        scores(1, b, j, t)
            elu_exps(BLOCKS - 1)
            mlp("dec", PARAMS.index("dec_mlp_b"))

            def keep_x2(i, c):
                act.wait_ge(x2_turned[c], i + 1 + START)
                act.activation(x2T[:, c].rearrange("p q n -> p (q n)"), psA[:, 2 * BANK:4 * BANK], ACT.Copy
                               ).then_inc(x2T_ready[c], 1)
                act.activation(x2[:, ds((2 * i + c) * CT, CT)], y[:, c], ACT.Copy).then_inc(x2_kept[c], 1)

            def keep_products(i, c, last):
                ch = 2 * i + c
                act.wait_ge(prod_free[c], i + START)
                act.wait_ge(q_lo, ch + START)
                for t in range(CT):
                    src = psB[:, 2 * (t % 2) * BANK:2 * (t % 2 + 1) * BANK]
                    act.wait_ge(prod_mm, ch * CT + t + 1)
                    act.activation(products[c][:, t], src[:, 0:HOPS * F], ACT.Copy)
                    act.activation(product3[:, t], src[:, HOPS * F:], ACT.Copy).then_inc(prod_copied, 1)
                    if t == 1 and not (last and c):
                        keep_x2(i + c, 1 - c)

            keep_x2(0, 0)
            with act.Fori(0, CHUNKS // 2 - 1) as i:
                for c in range(2):
                    keep_products(i, c, False)
            for c in range(2):
                keep_products(CHUNKS // 2 - 1, c, True)

            for n in range(HOPS):
                with act.Fori(0, APP) as u:
                    for s in range(2):
                        act.wait_ge(hop_adj_in[s], 16 * (n * APP + u + 1))
                        act.wait_ge(hop_contracted[s], n * APP + u + START)
                        act.activation(adjr[:, s].rearrange("p t x -> p (t x)"), adj8[:, s], ACT.Copy
                                       ).then_inc(cast_done[s], 1)

        @block.vector
        def _(dve):
            small = [0]

            def link(ins):
                small[0] += 1
                ins.then_inc(dve_small, 1)
                dve.wait_ge(dve_small, small[0])

            dve.memset(wT_sb[:], 0.0).then_inc(weights_zeroed, 1)
            dve.memset(w_sb[:], 0.0).then_inc(weights_zeroed, 1)
            dve.wait_ge(started, 1)
            dve.memset(ones[:], 1.0)
            dve.memset(minus_half[:], -0.5).then_inc(consts_set, 1)
            link(dve.memset(spread[:], 0.0))
            for k in range(2):
                for hh in range(2):
                    g = 32 * (2 * hh + k)
                    ins = dve.memset(spread[g:g + 1, k, D * hh:D * (hh + 1)], 1.0)
            link(ins)
            link(dve.memset(wv_cols[:], 0.0))
            dve.wait_ge(wv_mm, 1)
            link(dve.tensor_copy(wv[:], psB[:, 0:PAIRS]))
            for h in range(H):
                a = slice(D * (h % 2), D * (h % 2 + 1))
                ins = dve.tensor_scalar(wv_cols[a, h // 2, 32 * h:32 * h + 32], ones[a, :],
                                        wv[a, h // 2:h // 2 + 1], None,
                                        ALU.mult)
            ins.then_inc(wv_ready, 1)

            dve.wait_ge(weights_in, SETUP_LOADS)
            for half in range(2):
                with dve.Fori(half * CHUNKS // 4, (half + 1) * CHUNKS // 4) as i:
                    for c in range(2):
                        here = ds((2 * i + c) * CT, CT)
                        if half:
                            dve.wait_ge(f1_mm[c], i + 1)
                            dve.wait_ge(f1_stored[c], 16 * i + START)
                            dve.tensor_copy(f1_stage[:, c], psB[:, c * BANK:(c + 1) * BANK]).then_inc(f1_staged[c], 1)
                            dve.wait_ge(set_mm[c], i + 1 + START)
                            dve.tensor_copy(values[:, here, :].rearrange("p t f -> p (t f)"), chunk_ps[c]
                                            ).then_inc(set_copied[c], 1)
                        dve.wait_ge(set_copied[c], i + 1 + START)
                        dve.wait_ge(f2_sum[c], i + START)
                        dve.tensor_tensor(prod[:, c], values[:, here, :], v2_b[:].unsqueeze(1).to_broadcast([P, CT, F]),
                                          ALU.mult).then_inc(f2_prod[c], 1)
                        dve.wait_ge(f2_prod[c], i + 1)
                        dve.tensor_reduce(f2_half[:, here, :], prod[:, c].rearrange("p t (h e) -> p t h e", h=H),
                                          mybir.AxisListType.X, ALU.add).then_inc(f2_sum[c], 1)
                        dve.wait_ge(f2_sum[c], i + 1 + START)
                        dve.tensor_scalar(f2_half[:, here, :], f2_half[:, here, :], 0.5, None, ALU.mult
                                          ).then_inc(f2_ready, 1)

            def mask_scores(a, use, t, m):
                for hh in range(2):
                    if a == 0:
                        dve.wait_ge(exp_done[t], use + 1)
                    else:
                        dve.wait_ge(exp_done[t], APP + 2 * (use - APP) + hh + 1)
                    dve.tensor_tensor(ring[:, t, hh], ring[:, t, hh], m, ALU.mult).then_inc(masked[t], 1)

            def keep_lhs(use, t, j, q):
                dve.wait_ge(contracted[t], use + START)
                dve.tensor_copy(lhs[:, t:t + 1], values[:, ds(j * STEPS + t, 1), q * P:(q + 1) * P]
                                ).then_inc(lhs_ready[t], 1)

            def bn_coefficients(g, b):
                for q in range(PAIRS):
                    ins = dve.bn_aggr(moments[:, q], stats[:, q].rearrange("p c s -> p (c s)"))
                link(ins)
                dve.tensor_scalar(norm[:, 0], moments[:, :, 1], BN_EPS, None, ALU.add).then_inc(var_ready, 1)
                bn_coefficients.n += 1
                dve.wait_ge(rstd_ready, bn_coefficients.n)
                link(dve.tensor_tensor(norm[:, 2], norm[:, 1], par[:, g], ALU.mult))
                link(dve.tensor_tensor(norm[:, 0], moments[:, :, 0], norm[:, 2], ALU.mult))
                dve.tensor_tensor(norm[:, 3], par[:, b], norm[:, 0], ALU.subtract).then_inc(coefficients_ready, 1)
                dve.wait_ge(coefficients_ready, bn_coefficients.n)
            bn_coefficients.n = 0

            def apply_bn(dst, ch, done):
                for q in range(PAIRS):
                    ins = dve.tensor_scalar(dst[:, q], hT[:, q, ds(ch * CHUNK, CHUNK)], norm[:, 2, q:q + 1],
                                            norm[:, 3, q:q + 1], ALU.mult, ALU.add)
                ins.then_inc(done, 1)

            def mlp(tag):
                s = chunk[tag]

                def mix(i, c):
                    ch = 2 * i + c
                    here = hT[:, :, ds(ch * CHUNK, CHUNK)]
                    dve.wait_ge(s["act"][c], i + 1 + START)
                    dve.scalar_tensor_tensor(out=cexp[:, c], in0=cexp[:, c], scalar=1.0, in1=here,
                                             op0=ALU.min, op1=ALU.add).then_inc(s["mixed"][c], 1)
                    dve.wait_ge(s["mixed"][c], i + 1)
                    dve.scalar_tensor_tensor(out=here, in0=cexp[:, c], scalar=-1.0, in1=crelu[:, c],
                                             op0=ALU.add, op1=ALU.add).then_inc(s["h"][c], 1)
                    dve.wait_ge(s["h"][c], i + 1 + START)
                    for q in range(PAIRS):
                        ins = dve.bn_stats(stats[:, q, ds(ch, 1)].rearrange("p a s -> p (a s)"),
                                           hT[:, q, ds(ch * CHUNK, CHUNK)])
                    ins.then_inc(stats_done, 1)

                with dve.Fori(0, CHUNKS // 2) as i:
                    mix(i, 0)
                    mix(i, 1)

            def read_sums(b):
                half, q = b // PAIRS, b % PAIRS
                dve.wait_ge(contracted[STEPS - 1], (b + 1) * ITERS + START)
                dve.tensor_copy(hT[:, q, half * SPAN:(half + 1) * SPAN], psA[:, :]).then_inc(sums_copied, 1)
                dve.tensor_scalar(inv_den[:], den, 1e-30, None, ALU.max).then_inc(evacuated, 1)
                dve.wait_ge(evacuated, b + 1)

            def invert(r):
                at = slice(r * BANK, (r + 1) * BANK)
                dve.reciprocal(inv_den[:, at], inv_den[:, at]).then_inc(inv_ready, 1)

            def keep_inv(b, r):
                if b and r == 0:
                    dve.wait_ge(inv_stored, 16 * b)
                dve.wait_ge(spread_done, 2 * b + r + 1)
                dve.tensor_copy(inv_blk[:, 2 * r * BANK:2 * (r + 1) * BANK], spread_ps).then_inc(inv_copied, 1)

            def scale_sums(b):
                half, q = b // PAIRS, b % PAIRS
                here = hT[:, q, half * SPAN:(half + 1) * SPAN]
                dve.wait_ge(inv_copied, 2 * b + 2)
                dve.wait_ge(sums_copied, b + 1)
                dve.tensor_tensor(here, here, inv_blk[:], ALU.mult).then_inc(scaled, 1)

            def block_stats(b, quarters, count=None):
                half, q = b // PAIRS, b % PAIRS
                dve.wait_ge(scaled, count or b + 1)
                for k in quarters:
                    at = half * SPAN + k * BANK
                    dve.bn_stats(stats[:, q, half * QUARTERS + k], hT[:, q, at:at + BANK]).then_inc(stats_done, 1)

            end_parts = [read_sums, lambda b: invert(0), lambda b: invert(1), lambda b: keep_inv(b, 0),
                         lambda b: keep_inv(b, 1), scale_sums, lambda b: block_stats(b, (0, 1)),
                         lambda b: block_stats(b, (2, 3))]

            dve.wait_ge(dve_small, small[0])

            def take_bytes(b, j, t):
                n, use = b // PAIRS * ITERS + j, b * ITERS + j
                dve.wait_ge(adj_in[t], 16 * (n + 1))
                if t < 2:
                    dve.wait_ge(adj8_out[t + 2], 16 * n + START)
                    if b or not isinstance(j, int) or j:
                        dve.wait_ge(masked[t + 2], 2 * use)
                else:
                    dve.wait_ge(adj8_out[t - 2], 16 * (n + 1) + START)
                    dve.wait_ge(masked[t - 2], 2 * use + 2)
                dve.tensor_copy(mask8[:, t % 2], mask[:, t % 2]).then_inc(adj8_ready[t], 1)

            def first(b, j, t, last=False):
                half, q = b // PAIRS, b % PAIRS
                use = b * ITERS + j
                keep_lhs(use, t, j, q)
                if q == 0:
                    if t < STEPS - 1:
                        take_bytes(b, j, t + 1)
                    elif not last:
                        take_bytes(b, j + 1, 0)
                    dve.wait_ge(adj8_ready[t], half * ITERS + j + 1)
                else:
                    dve.wait_ge(mask_in[t], 16 * (half * ITERS + j + 1))
                mask_scores(0, use, t, mask8[:, t % 2])

            for b in range(BLOCKS):
                if b % PAIRS == 0:
                    take_bytes(b, 0, 0)
                for u, part in enumerate(end_parts):
                    first(b, u // STEPS, u % STEPS)
                    if b:
                        part(b - 1)
                with dve.Fori(len(end_parts) // STEPS, ITERS - 1) as j:
                    for t in range(STEPS):
                        first(b, j, t)
                for t in range(STEPS):
                    first(b, ITERS - 1, t, last=True)
            b = BLOCKS - 1
            q = b % PAIRS
            dve.wait_ge(contracted[STEPS - 1], APP + START)
            dve.tensor_scalar(inv_den[:], den, 1e-30, None, ALU.max).then_inc(evacuated, 1)
            dve.wait_ge(evacuated, BLOCKS)
            invert(0)
            invert(1)
            for r in range(2):
                keep_inv(b, r)
                dve.wait_ge(inv_copied, 2 * b + r + 1)
                part = slice(2 * r * BANK, 2 * (r + 1) * BANK)
                at = b // PAIRS * SPAN
                dve.tensor_tensor(hT[:, q, at + part.start:at + part.stop], psA[:, part], inv_blk[:, part], ALU.mult
                                  ).then_inc(scaled, 1)
                block_stats(b, (2 * r, 2 * r + 1), b + r + 1)
            dve.wait_ge(stats_done, BLOCKS * QUARTERS)
            dve.wait_ge(weights_in, SETUP_LOADS + 3 * 16)

            bn_coefficients(PARAMS.index("enc_g"), PARAMS.index("enc_b"))
            mlp("enc")
            dve.wait_ge(stats_done, BLOCKS * QUARTERS + CHUNKS)
            bn_coefficients(PARAMS.index("enc_mlp_g"), PARAMS.index("enc_mlp_beta"))
            for k in range(2):
                with dve.Fori(k * CHUNKS // 4, (k + 1) * CHUNKS // 4) as i:
                    for c in range(2):
                        dve.wait_ge(chunk["emb"]["mm"][c], i + START)
                        apply_bn(cin[:, c], 2 * i + c, chunk["emb"]["cin"][c])
                dve.wait_ge(mask_in[2 * k], 16 * (HALVES * ITERS + 1))
                mask_scores(1, APP, 2 * k, mask8[:, k])
            for c in range(2):
                dve.wait_ge(chunk["emb"]["act"][c], CHUNKS // 2 + START)

            def second(b, j, t):
                use = APP + b * ITERS + j
                keep_lhs(use, t, j, b % PAIRS)
                if t % 2 == 0 and (b or not isinstance(j, int) or j):
                    dve.wait_ge(mask_in[t], 16 * (HALVES * ITERS + b * ITERS + j + 1))
                    mask_scores(1, use, t, mask8[:, t // 2])

            def scale_second(b):
                half, q = b // PAIRS, b % PAIRS
                dve.wait_ge(inv_in, 16 * (b + 1))
                dve.wait_ge(contracted[STEPS - 1], APP + (b + 1) * ITERS + START)
                dve.tensor_tensor(hT[:, q, half * SPAN:(half + 1) * SPAN], (psA, psB)[b % 2][:, :], inv_blk[:], ALU.mult
                                  ).then_inc(evacuated, 1)
                dve.wait_ge(evacuated, BLOCKS + b + 1)

            def elu(b):
                half, q = b // PAIRS, b % PAIRS
                here = hT[:, q, half * SPAN:(half + 1) * SPAN]
                dve.wait_ge(elu_exp, b + 1)
                dve.tensor_scalar(inv_blk[:], inv_blk[:], 1.0, -1.0, ALU.min, ALU.add).then_inc(elu_min, 1)
                dve.wait_ge(elu_min, b + 1)
                dve.scalar_tensor_tensor(out=here, in0=here, scalar=0.0, in1=inv_blk[:], op0=ALU.max, op1=ALU.add
                                         ).then_inc(elu_done, 1)

            for b in range(BLOCKS):
                for t in range(STEPS):
                    second(b, 0, t)
                    if b and t == 0:
                        scale_second(b - 1)
                if b:
                    elu(b - 1)
                with dve.Fori(1, ITERS) as j:
                    for t in range(STEPS):
                        second(b, j, t)
            scale_second(BLOCKS - 1)
            elu(BLOCKS - 1)
            dve.wait_ge(elu_done, BLOCKS)
            mlp("dec")
            dve.wait_ge(stats_done, BLOCKS * QUARTERS + 2 * CHUNKS)
            bn_coefficients(PARAMS.index("dec_mlp_g"), PARAMS.index("dec_mlp_beta"))

            def layernorm(n, src, dst, done):
                for t in range(CT):
                    ins = dve.bn_stats(ln_stats[:, t], src[:, t])
                ins.then_inc(ln_small_done, 1)
                dve.wait_ge(ln_small_done, 3 * n + 1)
                dve.memset(ln_gate[:], 0.0)
                for t in range(CT):
                    ins = dve.bn_aggr(ln_mom[:, t], ln_stats[:, t])
                ins.then_inc(ln_small_done, 1)
                dve.wait_ge(ln_small_done, 3 * n + 2)
                dve.tensor_scalar(ln_small[:, 0], ln_mom[:, :, 1], LN_EPS, None, ALU.add).then_inc(ln_var, 1)
                dve.wait_ge(ln_rstd, n + 1)
                dve.scalar_tensor_tensor(out=ln_small[:, 2], in0=ln_mom[:, :, 0], scalar=-1.0, in1=ln_small[:, 1],
                                         op0=ALU.mult, op1=ALU.mult).then_inc(ln_small_done, 1)
                dve.wait_ge(ln_small_done, 3 * n + 3)
                for t in range(CT):
                    ins = dve.tensor_scalar(dst[:, t], src[:, t], ln_small[:, 1, t:t + 1], ln_small[:, 2, t:t + 1],
                                            ALU.mult, ALU.add)
                ins.then_inc(done, 1)

            def norm_and_sum(i, c):
                ch = 2 * i + c
                dve.wait_ge(turned[c], i + START)
                apply_bn(normed[:, c], ch, normed_ready[c])
                dve.wait_ge(turned[c], i + 1 + START)
                dve.wait_ge(x_in[c], 16 * (i + 1))
                dve.wait_ge(x2_turned[c], i + START)
                dve.wait_ge(x2_kept[c], i + START)
                dve.tensor_tensor(y[:, c], psA[:, 0:2 * BANK].rearrange("p (t f) -> p t f", t=CT), xin[:, c], ALU.add
                                  ).then_inc(summed[c], 1)
                dve.wait_ge(summed[c], i + 1 + START)
                layernorm(ch, y[:, c], y[:, c], x2_ready[c])

            def split(ch):
                dve.wait_ge(prod_copied, (ch + 1) * CT + START)
                src = product3[:]
                hi = q0[:, ds(ch * CT, CT), 0]
                lo = q0[:, ds(ch * CT, CT), 1]
                dve.tensor_copy(hi, src).then_inc(q_hi, 1)
                dve.wait_ge(q_hi, ch + 1)
                dve.tensor_tensor(lo, src, hi.bitcast(F32), ALU.subtract).then_inc(q_lo, 1)

            norm_and_sum(0, 0)
            norm_and_sum(0, 1)
            with dve.Fori(0, CHUNKS // 2 - 1) as i:
                for c in range(2):
                    norm_and_sum(i + 1, c)
                    split(2 * i + c)
            split(CHUNKS - 2)
            split(CHUNKS - 1)

            for n in range(HOPS):
                last = n == HOPS - 1
                dst = (q1, q0)[n % 2]
                with dve.Fori(0, BLOCKS) as ib:
                    for c in range(2):
                        b = n * 2 * BLOCKS + 2 * ib + c
                        acc = (psA, psB)[c][:, :].rearrange("p (m k f) -> p m k f", m=CT, k=2)
                        dve.wait_ge(xw_in[c], 16 * (n * BLOCKS + ib + 1))
                        dve.wait_ge(hop_contracted[1], n * APP + ib * ITERS + (c + 1) * (ITERS // 2) + START)
                        if last:
                            dve.wait_ge(out_free, 2 * ib + c + START)
                        dve.tensor_tensor(xw[:, c], acc[:, :, 1], xw[:, c], ALU.add).then_inc(sum1, 1)
                        dve.wait_ge(sum1, b + 1)
                        dve.tensor_tensor(total[:], acc[:, :, 0], xw[:, c], ALU.add).then_inc(hop_evac[c], 1)
                        dve.wait_ge(hop_evac[c], n * BLOCKS + ib + 1 + START)
                        here = ds((2 * ib + c) * CT, CT)
                        if not last:
                            dve.tensor_copy(dst[:, here, 0], total[:]).then_inc(hop_hi, 1)
                            dve.wait_ge(hop_hi, b + 1)
                            dve.tensor_tensor(dst[:, here, 1], total[:], dst[:, here, 0].bitcast(F32), ALU.subtract
                                              ).then_inc(hop_q, 1)
                        else:
                            dve.tensor_tensor(total[:], total[:], x2[:, here], ALU.add).then_inc(sum2, 1)
                            dve.wait_ge(sum2, 2 * ib + c + 1)
                            layernorm(CHUNKS + 2 * ib + c, total, total, out_ready)

        @block.gpsimd
        def _(pool):
            for s in reused:
                pool.sem_inc(s, START)
            pool.sem_inc(started, 1)
            pool.memset(ident[:], 0.0).then_inc(ident0, 1)
            pool.wait_ge(ident0, 1)
            pool.affine_select(out=ident[:], in_=ident[:], compare_op=ALU.not_equal, fill=1.0, base=0,
                               pattern=[[-1, P]], channel_multiplier=1).then_inc(ident_set, 1)
            pool.wait_ge(consts_set, 1)

            def bn_pow(n):
                pool.wait_ge(var_ready, n + 1)
                pool.tensor_tensor(norm[:, 1], norm[:, 0], minus_half[:, 0:PAIRS], ALU.pow).then_inc(rstd_ready, 1)

            bn_pow(0)
            bn_pow(1)
            bn_pow(2)

            def ln_pow(n):
                pool.wait_ge(ln_var, n + 1)
                pool.tensor_tensor(ln_small[:, 1], ln_small[:, 0], minus_half[:], ALU.pow).then_inc(ln_rstd, 1)

            ln_pow(0)

            def store_products(i, c):
                ch = 2 * i + c
                pool.wait_ge(prod_copied, (ch + 1) * CT + START)
                pool.dma_start(xw_dram[ds(ch * CT, CT)].rearrange("t p k f -> p t (k f)"), products[c][:]
                               ).then_inc(prod_stored, 16)

            def free_products(i, c):
                pool.wait_ge(prod_stored, 16 * (2 * i + c + 1))
                pool.sem_inc(prod_free[c], 1)

            ln_pow(1)
            ln_pow(2)
            store_products(0, 0)
            ln_pow(3)
            free_products(0, 0)
            store_products(0, 1)
            with pool.Fori(1, CHUNKS // 2 - 1) as i:
                ln_pow(2 * i + 2)
                free_products(i - 1, 1)
                store_products(i, 0)
                ln_pow(2 * i + 3)
                free_products(i, 0)
                store_products(i, 1)
            i = CHUNKS // 2 - 1
            free_products(i - 1, 1)
            store_products(i, 0)
            free_products(i, 0)
            store_products(i, 1)
            free_products(i, 1)
            with pool.Fori(0, CHUNKS) as b:
                ln_pow(CHUNKS + b)
                pool.wait_ge(out_ready, b + 1)
                pool.dma_start(out_view[ds(b, 1)].rearrange("a p t f -> p (a t) f"), total[:]).then_inc(out_stored, 16)
                pool.wait_ge(out_stored, 16 * (b + 1))
                pool.sem_inc(out_free, 1)


def kernel(**inputs):
    import numpy as np
    import concourse.bacc as bacc
    from concourse.bass_utils import run_bass_kernel_spmd

    g = {k.replace("L0_gnn_", ""): np.asarray(v) for k, v in inputs.items()}
    pairs = lambda a: np.ascontiguousarray(a.reshape(PAIRS, 2 * D, -1).transpose(1, 0, 2))
    vec = [g[k] for k in ("enc_bn_gamma", "enc_bn_beta", "enc_mlp_b", "enc_mlp_bn_gamma", "enc_mlp_bn_beta",
                          "dec_mlp_b", "dec_mlp_bn_gamma", "dec_mlp_bn_beta")]
    W, V = g["W"], g["V"]
    arrays = {
        "x": np.ascontiguousarray(g["x"]),
        "xT": np.ascontiguousarray(g["x"].T),
        "adjT": np.ascontiguousarray(
            g["adj"].reshape(HALVES, SPAN, NT, P).transpose(0, 2, 3, 1).reshape(HALVES * NT, P, SPAN)),
        "head_w": pairs(W),
        "head_wT": pairs(np.ascontiguousarray(W.transpose(0, 2, 1))),
        "v1": np.ascontiguousarray(V[:, 0, :, 0].reshape(PAIRS, P).T),
        "v2_row": np.ascontiguousarray(V[:, 1, :, 0].reshape(F)),
        "params": np.ascontiguousarray(np.stack(vec).reshape(len(vec), PAIRS, P).transpose(2, 0, 1)),
        "enc_wT": np.ascontiguousarray(g["enc_mlp_W"].T.reshape(PAIRS, P, F).transpose(1, 0, 2)),
        "dec_wT": np.ascontiguousarray(g["dec_mlp_W"].T.reshape(PAIRS, P, F).transpose(1, 0, 2)),
        "hop_w": np.ascontiguousarray(g["L1_gnn_weight"].reshape(4, PAIRS, P, F).transpose(2, 1, 0, 3)),
    }
    nc = bacc.Bacc("TRN2", target_bir_lowering=False, num_devices=1)
    aps = [nc.dram_tensor(f"in_{k}", a.shape, mybir.dt.from_np(a.dtype), kind="ExternalInput").ap()
           for k, a in arrays.items()]
    out = nc.dram_tensor("out_dram", [N, F], F32, kind="ExternalOutput").ap()
    gnn_kernel(nc, *aps, out)
    r = run_bass_kernel_spmd(nc, [{f"in_{k}": a for k, a in arrays.items()}], core_ids=[0])
    return r.results[0]["out_dram"]
```
